# Optimizing a Trainium2 kernel written in Bass

```python
import numpy as np
import jax
import jax.numpy as jnp

def _softmax(x, axis=-1):
    return jax.nn.softmax(x, axis=axis)

def _gelu(x):
    return jax.nn.gelu(x, approximate=True)

def _silu(x):
    return jax.nn.silu(x)

def _sigmoid(x):
    return jax.nn.sigmoid(x)

def _layernorm(x, axis=-1, eps=1e-05):
    m = jnp.mean(x, axis=axis, keepdims=True)
    v = jnp.var(x, axis=axis, keepdims=True)
    return (x - m) / jnp.sqrt(v + eps)

def _scatter_add(tgt, idx, src, axis=0):
    return tgt.at[idx].add(src)

def _segment_sum(src, seg, n):
    return jax.ops.segment_sum(src, seg, n)
kernel_name = 'mk_decoder_postln_d2_seqx_r8_d8e2f5'

def setup_inputs(seed: int=0):
    np.random.seed(seed)
    _w = jnp.asarray

    def _rec_inputs():
        import jax
        import jax.numpy as jnp
        _rk = jax.random.key(seed)
        x = 7.22e-05 + 1 * jax.random.normal(jax.random.fold_in(_rk, 1), (128, 64, 128), jnp.float32)
        _lenS = 64 - jax.random.randint(jax.random.fold_in(_rk, 7), (128,), 0, max(1, 64 // 4) + 1, jnp.int32)
        _lenS2 = 64 - jax.random.randint(jax.random.fold_in(_rk, 8), (128,), 0, max(1, 64 // 4) + 1, jnp.int32)
        _ctx_1024P = jax.random.normal(jax.random.fold_in(_rk, 11), (128, 16, 128), jnp.float32)
        _ctx_1024c = jax.random.dirichlet(jax.random.fold_in(_rk, 511), 0.3 * jnp.ones((16,), jnp.float32), (128, 64))
        _ctx_1024t = jnp.einsum('bsk,bkd->bsd', _ctx_1024c, _ctx_1024P)
        _ctx_1024t = _ctx_1024t * jax.lax.rsqrt(jnp.mean(jnp.square(_ctx_1024t)) + 1e-12) * 0.953939
        ctx_1024 = 4.13588e-05 + 0.999923 * (_ctx_1024t + 0.3 * jax.random.normal(jax.random.fold_in(_rk, 611), (128, 64, 128), jnp.float32))
        return (x, ctx_1024)
    x, ctx_1024 = _rec_inputs()

    def _L0_attn_setup():
        import jax, jax.numpy as jnp
        import numpy as np
        FEATS = 128
        HEAD = 16
        HEAD_DIM = FEATS // HEAD
        EPS = 1e-12

        def _l2norm(t):
            n = jnp.sqrt(jnp.sum(t * t, axis=-1, keepdims=True))
            return t / jnp.maximum(n, EPS)
        key = jax.random.key(seed)
        ks = jax.random.split(key, 10)
        s = 0.02
        inp = {'x': jax.random.normal(ks[0], (4, 256, FEATS), dtype=jnp.float32), 'Wq': jax.random.normal(ks[1], (FEATS, FEATS), dtype=jnp.float32) * s, 'bq': jnp.zeros((FEATS,), dtype=jnp.float32), 'Wk': jax.random.normal(ks[2], (FEATS, FEATS), dtype=jnp.float32) * s, 'bk': jnp.zeros((FEATS,), dtype=jnp.float32), 'Wv': jax.random.normal(ks[3], (FEATS, FEATS), dtype=jnp.float32) * s, 'bv': jnp.zeros((FEATS,), dtype=jnp.float32), 'Wo': jax.random.normal(ks[4], (FEATS, FEATS), dtype=jnp.float32) * s, 'bo': jnp.zeros((FEATS,), dtype=jnp.float32), 'm': jnp.full((HEAD,), 0.5, dtype=jnp.float32)}
        return inp
    _L0_attn_all = _L0_attn_setup()
    _L0_attn_in = {k: v for k, v in _L0_attn_all.items() if k in ('Wq', 'bq', 'Wk', 'bk', 'Wv', 'bv', 'Wo', 'bo', 'm')}
    del _L0_attn_all

    def _L0_xattn_setup():
        import jax, jax.numpy as jnp
        import numpy as np
        D = 128
        H = 16
        HD = D // H
        key = jax.random.key(seed)
        ks = jax.random.split(key, 11)
        B, T = (4, 256)
        s = 1.0 / np.sqrt(D)
        inp = {'q': jax.random.normal(ks[0], (B, T, D), jnp.float32), 'k': jax.random.normal(ks[1], (B, T, D), jnp.float32), 'v': jax.random.normal(ks[2], (B, T, D), jnp.float32), 'Wq': jax.random.normal(ks[3], (D, D), jnp.float32) * s, 'bq': jnp.zeros((D,), jnp.float32), 'Wk': jax.random.normal(ks[4], (D, D), jnp.float32) * s, 'bk': jnp.zeros((D,), jnp.float32), 'Wv': jax.random.normal(ks[5], (D, D), jnp.float32) * s, 'bv': jnp.zeros((D,), jnp.float32), 'Wo': jax.random.normal(ks[6], (D, D), jnp.float32) * s, 'bo': jnp.zeros((D,), jnp.float32)}
        return inp
    _L0_xattn_all = _L0_xattn_setup()
    _L0_xattn_in = {k: v for k, v in _L0_xattn_all.items() if k in ('Wq', 'bq', 'Wk', 'bk', 'Wv', 'bv', 'Wo', 'bo')}
    del _L0_xattn_all

    def _L0_ffn_setup():
        import jax, jax.numpy as jnp
        import numpy as np
        NUM_EXPERTS = 8
        CAPACITY = 80
        key = jax.random.key(seed)
        ks = jax.random.split(key, 5)
        D, E, F = (128, NUM_EXPERTS, 512)
        inputs = jax.random.normal(ks[0], (2, 256, D), dtype=jnp.float32)
        gate_w = jax.random.normal(ks[1], (D, E), dtype=jnp.float32) * 0.02
        gate_b = jnp.zeros((E,), dtype=jnp.float32)
        w1 = jax.random.normal(ks[2], (E, D, F), dtype=jnp.float32) * 0.02
        b1 = jnp.zeros((E, F), dtype=jnp.float32)
        w2 = jax.random.normal(ks[3], (E, F, D), dtype=jnp.float32) * 0.02
        b2 = jnp.zeros((E, D), dtype=jnp.float32)
        return {'inputs': inputs, 'gate_w': gate_w, 'gate_b': gate_b, 'w1': w1, 'b1': b1, 'w2': w2, 'b2': b2}
    _L0_ffn_all = _L0_ffn_setup()
    _L0_ffn_in = {k: v for k, v in _L0_ffn_all.items() if k in ('gate_w', 'gate_b', 'w1', 'b1', 'w2', 'b2')}
    del _L0_ffn_all

    def _L1_attn_setup():
        import jax, jax.numpy as jnp
        import numpy as np
        N_EMBD = 128
        N_HEAD = 16
        LATENT = 64
        HEAD_DIM = N_EMBD // N_HEAD
        B, T = (2, 256)
        SCALE = 1.0 / np.sqrt(LATENT)
        key = jax.random.key(seed)
        ks = jax.random.split(key, 10)
        s = lambda fan_in: 1.0 / np.sqrt(fan_in)
        return {'x': jax.random.normal(ks[0], (B, T, N_EMBD), dtype=jnp.float32), 'Wq': jax.random.normal(ks[1], (N_EMBD, N_EMBD), dtype=jnp.float32) * s(N_EMBD), 'bq': jnp.zeros((N_EMBD,), dtype=jnp.float32), 'Wk': jax.random.normal(ks[2], (N_EMBD, N_HEAD * LATENT), dtype=jnp.float32) * s(N_EMBD), 'bk': jnp.zeros((N_HEAD * LATENT,), dtype=jnp.float32), 'Wv': jax.random.normal(ks[3], (N_EMBD, N_HEAD * LATENT), dtype=jnp.float32) * s(N_EMBD), 'bv': jnp.zeros((N_HEAD * LATENT,), dtype=jnp.float32), 'Wo': jax.random.normal(ks[4], (N_HEAD * LATENT, N_EMBD), dtype=jnp.float32) * s(N_HEAD * LATENT), 'bo': jnp.zeros((N_EMBD,), dtype=jnp.float32), 'Wc': jax.random.normal(ks[5], (HEAD_DIM, LATENT), dtype=jnp.float32) * s(HEAD_DIM)}
    _L1_attn_all = _L1_attn_setup()
    _L1_attn_in = {k: v for k, v in _L1_attn_all.items() if k in ('Wq', 'bq', 'Wk', 'bk', 'Wv', 'bv', 'Wo', 'bo', 'Wc')}
    del _L1_attn_all

    def _L1_xattn_setup():
        import jax, jax.numpy as jnp
        import numpy as np
        D_MODEL = 128
        NUM_HEADS = 16
        HEAD_DIM = D_MODEL // NUM_HEADS
        B, S = (4, 256)

        def _split_heads(x):
            b, s, _ = x.shape
            return x.reshape(b, s, NUM_HEADS, HEAD_DIM).transpose(0, 2, 1, 3)
        key = jax.random.key(seed)
        ks = jax.random.split(key, 11)
        sc = 1.0 / np.sqrt(D_MODEL)
        return {'query': jax.random.normal(ks[0], (B, S, D_MODEL), jnp.float32), 'key': jax.random.normal(ks[1], (B, S, D_MODEL), jnp.float32), 'value': jax.random.normal(ks[2], (B, S, D_MODEL), jnp.float32), 'Wq': jax.random.normal(ks[3], (D_MODEL, D_MODEL), jnp.float32) * sc, 'bq': jnp.zeros((D_MODEL,), jnp.float32), 'Wk': jax.random.normal(ks[4], (D_MODEL, D_MODEL), jnp.float32) * sc, 'bk': jnp.zeros((D_MODEL,), jnp.float32), 'Wv': jax.random.normal(ks[5], (D_MODEL, D_MODEL), jnp.float32) * sc, 'bv': jnp.zeros((D_MODEL,), jnp.float32), 'Wo': jax.random.normal(ks[6], (D_MODEL, D_MODEL), jnp.float32) * sc, 'bo': jnp.zeros((D_MODEL,), jnp.float32)}
    _L1_xattn_all = _L1_xattn_setup()
    _L1_xattn_in = {k: v for k, v in _L1_xattn_all.items() if k in ('Wq', 'bq', 'Wk', 'bk', 'Wv', 'bv', 'Wo', 'bo')}
    del _L1_xattn_all

    def _L1_ffn_setup():
        import jax, jax.numpy as jnp
        import numpy as np
        B, T, D, E, H = (8, 256, 128, 8, 32)
        LN_EPS = 1e-05
        key = jax.random.key(seed)
        ks = jax.random.split(key, 4)
        return {'x': jax.random.normal(ks[0], (B, T, D), dtype=jnp.float32), 'Wg': jax.random.normal(ks[1], (E, D), dtype=jnp.float32) * 0.02, 'ln_scale': jnp.ones((E, D), dtype=jnp.float32), 'ln_bias': jnp.zeros((E, D), dtype=jnp.float32), 'W1': jax.random.normal(ks[2], (E, D, H), dtype=jnp.float32) * 0.02, 'b1': jnp.zeros((E, H), dtype=jnp.float32), 'W2': jax.random.normal(ks[3], (E, H, D), dtype=jnp.float32) * 0.02, 'b2': jnp.zeros((E, D), dtype=jnp.float32)}
    _L1_ffn_all = _L1_ffn_setup()
    _L1_ffn_in = {k: v for k, v in _L1_ffn_all.items() if k in ('Wg', 'ln_scale', 'ln_bias', 'W1', 'b1', 'W2', 'b2')}
    del _L1_ffn_all
    return {'x': x, 'ctx_1024': ctx_1024, 'L0_attn_Wq': _L0_attn_in['Wq'], 'L0_attn_bq': _L0_attn_in['bq'], 'L0_attn_Wk': _L0_attn_in['Wk'], 'L0_attn_bk': _L0_attn_in['bk'], 'L0_attn_Wv': _L0_attn_in['Wv'], 'L0_attn_bv': _L0_attn_in['bv'], 'L0_attn_Wo': _L0_attn_in['Wo'], 'L0_attn_bo': _L0_attn_in['bo'], 'L0_attn_m': _L0_attn_in['m'], 'L0_xattn_Wq': _L0_xattn_in['Wq'], 'L0_xattn_bq': _L0_xattn_in['bq'], 'L0_xattn_Wk': _L0_xattn_in['Wk'], 'L0_xattn_bk': _L0_xattn_in['bk'], 'L0_xattn_Wv': _L0_xattn_in['Wv'], 'L0_xattn_bv': _L0_xattn_in['bv'], 'L0_xattn_Wo': _L0_xattn_in['Wo'], 'L0_xattn_bo': _L0_xattn_in['bo'], 'L0_ffn_gate_w': _L0_ffn_in['gate_w'], 'L0_ffn_gate_b': _L0_ffn_in['gate_b'], 'L0_ffn_w1': _L0_ffn_in['w1'], 'L0_ffn_b1': _L0_ffn_in['b1'], 'L0_ffn_w2': _L0_ffn_in['w2'], 'L0_ffn_b2': _L0_ffn_in['b2'], 'L1_attn_Wq': _L1_attn_in['Wq'], 'L1_attn_bq': _L1_attn_in['bq'], 'L1_attn_Wk': _L1_attn_in['Wk'], 'L1_attn_bk': _L1_attn_in['bk'], 'L1_attn_Wv': _L1_attn_in['Wv'], 'L1_attn_bv': _L1_attn_in['bv'], 'L1_attn_Wo': _L1_attn_in['Wo'], 'L1_attn_bo': _L1_attn_in['bo'], 'L1_attn_Wc': _L1_attn_in['Wc'], 'L1_xattn_Wq': _L1_xattn_in['Wq'], 'L1_xattn_bq': _L1_xattn_in['bq'], 'L1_xattn_Wk': _L1_xattn_in['Wk'], 'L1_xattn_bk': _L1_xattn_in['bk'], 'L1_xattn_Wv': _L1_xattn_in['Wv'], 'L1_xattn_bv': _L1_xattn_in['bv'], 'L1_xattn_Wo': _L1_xattn_in['Wo'], 'L1_xattn_bo': _L1_xattn_in['bo'], 'L1_ffn_Wg': _L1_ffn_in['Wg'], 'L1_ffn_ln_scale': _L1_ffn_in['ln_scale'], 'L1_ffn_ln_bias': _L1_ffn_in['ln_bias'], 'L1_ffn_W1': _L1_ffn_in['W1'], 'L1_ffn_b1': _L1_ffn_in['b1'], 'L1_ffn_W2': _L1_ffn_in['W2'], 'L1_ffn_b2': _L1_ffn_in['b2']}

def reference(x, ctx_1024, L0_attn_Wq, L0_attn_bq, L0_attn_Wk, L0_attn_bk, L0_attn_Wv, L0_attn_bv, L0_attn_Wo, L0_attn_bo, L0_attn_m, L0_xattn_Wq, L0_xattn_bq, L0_xattn_Wk, L0_xattn_bk, L0_xattn_Wv, L0_xattn_bv, L0_xattn_Wo, L0_xattn_bo, L0_ffn_gate_w, L0_ffn_gate_b, L0_ffn_w1, L0_ffn_b1, L0_ffn_w2, L0_ffn_b2, L1_attn_Wq, L1_attn_bq, L1_attn_Wk, L1_attn_bk, L1_attn_Wv, L1_attn_bv, L1_attn_Wo, L1_attn_bo, L1_attn_Wc, L1_xattn_Wq, L1_xattn_bq, L1_xattn_Wk, L1_xattn_bk, L1_xattn_Wv, L1_xattn_bv, L1_xattn_Wo, L1_xattn_bo, L1_ffn_Wg, L1_ffn_ln_scale, L1_ffn_ln_bias, L1_ffn_W1, L1_ffn_b1, L1_ffn_W2, L1_ffn_b2):
    import jax
    import jax.numpy as jnp

    def _L0_attn_ref(x, Wq, bq, Wk, bk, Wv, bv, Wo, bo, m):
        import jax, jax.numpy as jnp
        import numpy as np
        FEATS = 128
        HEAD = 16
        HEAD_DIM = FEATS // HEAD
        EPS = 1e-12

        def _l2norm(t):
            n = jnp.sqrt(jnp.sum(t * t, axis=-1, keepdims=True))
            return t / jnp.maximum(n, EPS)
        b, n, f = x.shape

        def proj(W, bias):
            y = x @ W + bias
            return y.reshape(b, n, HEAD, HEAD_DIM).transpose(0, 2, 1, 3)
        q = _l2norm(proj(Wq, bq))
        k = _l2norm(proj(Wk, bk))
        v = proj(Wv, bv)
        sim = jnp.einsum('bhid,bhjd->bhij', q, k)
        sigma_m = jax.nn.sigmoid(m).reshape(1, HEAD, 1, 1)
        scaling = jnp.asarray(n, dtype=x.dtype) ** sigma_m
        attn = sim / scaling
        out = jnp.einsum('bhij,bhjd->bhid', attn, v)
        out = out.transpose(0, 2, 1, 3).reshape(b, n, f)
        return out @ Wo + bo

    def _L0_xattn_ref(q, k, v, Wq, bq, Wk, bk, Wv, bv, Wo, bo):
        import jax, jax.numpy as jnp
        import numpy as np
        D = 128
        H = 16
        HD = D // H
        B, Tq, _ = q.shape
        Tk = k.shape[1]
        qw = q @ Wq + bq
        kw = k @ Wk + bk
        vw = v @ Wv + bv
        qh = qw.reshape(B, Tq, H, HD)
        kh = kw.reshape(B, Tk, H, HD)
        vh = vw.reshape(B, Tk, H, HD)
        scale = 1.0 / np.sqrt(HD).astype(np.float32)
        logits = jnp.einsum('bqhd,bkhd->bhqk', qh, kh) * scale
        causal = jnp.tril(jnp.ones((Tq, Tk), bool))
        logits = jnp.where(causal, logits, -jnp.inf)
        attn = jax.nn.softmax(logits, axis=-1)
        out = jnp.einsum('bhqk,bkhd->bqhd', attn, vh).reshape(B, Tq, D)
        return out @ Wo + bo

    def _L0_ffn_ref(inputs, gate_w, gate_b, w1, b1, w2, b2):
        import jax, jax.numpy as jnp
        import numpy as np
        NUM_EXPERTS = 8
        CAPACITY = 80
        D = inputs.shape[-1]
        tokens = inputs.reshape(-1, D)
        logits = tokens @ gate_w + gate_b
        probs = jax.nn.softmax(logits, axis=-1)
        expert_idx = jnp.argmax(probs, axis=-1)
        mask1 = jax.nn.one_hot(expert_idx, NUM_EXPERTS, dtype=jnp.float32)
        pos = jnp.sum(jnp.cumsum(mask1, axis=0) * mask1, axis=-1) - 1.0
        pos = pos.astype(jnp.int32)
        keep = (pos < CAPACITY).astype(jnp.float32)
        gate_prob = jnp.sum(probs * mask1, axis=-1)
        pos_oh = jax.nn.one_hot(pos, CAPACITY, dtype=jnp.float32)
        sec_mask = mask1[:, :, None] * pos_oh[:, None, :] * keep[:, None, None]
        combine_weights = sec_mask * gate_prob[:, None, None]
        dispatch = jnp.einsum('nec,nd->ecd', sec_mask, tokens)
        h = jax.nn.gelu(jnp.einsum('ecd,edf->ecf', dispatch, w1) + b1[:, None, :])
        expert_out = jnp.einsum('ecf,efd->ecd', h, w2) + b2[:, None, :]
        out = jnp.einsum('nec,ecd->nd', combine_weights, expert_out)
        return out.reshape(inputs.shape)

    def _L1_attn_ref(x, Wq, bq, Wk, bk, Wv, bv, Wo, bo, Wc):
        import jax, jax.numpy as jnp
        import numpy as np
        N_EMBD = 128
        N_HEAD = 16
        LATENT = 64
        HEAD_DIM = N_EMBD // N_HEAD
        B, T = (2, 256)
        SCALE = 1.0 / np.sqrt(LATENT)
        Bv, Tv, C = x.shape
        q = (x @ Wq + bq).reshape(Bv, Tv, N_HEAD, HEAD_DIM)
        k = (x @ Wk + bk).reshape(Bv, Tv, N_HEAD, LATENT)
        v = (x @ Wv + bv).reshape(Bv, Tv, N_HEAD, LATENT)
        qc = jnp.einsum('bthd,dl->bthl', q, Wc)
        att = jnp.einsum('bthl,bshl->bhts', qc, k) * SCALE
        causal = jnp.tril(jnp.ones((Tv, Tv), dtype=bool))
        att = jnp.where(causal[None, None], att, -jnp.inf)
        att = jax.nn.softmax(att, axis=-1)
        y = jnp.einsum('bhts,bshl->bthl', att, v).reshape(Bv, Tv, N_HEAD * LATENT)
        return y @ Wo + bo

    def _L1_xattn_ref(query, key, value, Wq, bq, Wk, bk, Wv, bv, Wo, bo):
        import jax, jax.numpy as jnp
        import numpy as np
        D_MODEL = 128
        NUM_HEADS = 16
        HEAD_DIM = D_MODEL // NUM_HEADS
        B, S = (4, 256)

        def _split_heads(x):
            b, s, _ = x.shape
            return x.reshape(b, s, NUM_HEADS, HEAD_DIM).transpose(0, 2, 1, 3)
        q = _split_heads(query @ Wq + bq)
        k = _split_heads(key @ Wk + bk)
        v = _split_heads(value @ Wv + bv)
        scores = jnp.einsum('bhqd,bhkd->bhqk', q, k) / np.sqrt(HEAD_DIM)
        attn = jax.nn.softmax(scores, axis=-1)
        out = jnp.einsum('bhqk,bhkd->bhqd', attn, v)
        out = out.transpose(0, 2, 1, 3).reshape(query.shape[0], -1, D_MODEL)
        return out @ Wo + bo

    def _L1_ffn_ref(x, Wg, ln_scale, ln_bias, W1, b1, W2, b2):
        import jax, jax.numpy as jnp
        import numpy as np
        B, T, D, E, H = (8, 256, 128, 8, 32)
        LN_EPS = 1e-05
        Bs, Ts, Ds = x.shape
        xt = x.reshape(Bs * Ts, Ds)
        logits = xt @ Wg.T
        top1 = jnp.argmax(logits, axis=-1)
        mu = jnp.mean(xt, axis=-1, keepdims=True)
        var = jnp.mean(jnp.square(xt - mu), axis=-1, keepdims=True)
        xhat = (xt - mu) * jax.lax.rsqrt(var + LN_EPS)
        n_experts = Wg.shape[0]

        def body(y, p):
            s_e, b_e, w1, bb1, w2, bb2, eid = p
            h = jax.nn.gelu((xhat * s_e + b_e) @ w1 + bb1, approximate=False)
            out = h @ w2 + bb2
            mask = (top1 == eid)[:, None].astype(out.dtype)
            return (y + mask * out, None)
        y0 = jnp.zeros_like(xt)
        y, _ = jax.lax.scan(body, y0, (ln_scale, ln_bias, W1, b1, W2, b2, jnp.arange(n_experts)))
        return y.reshape(Bs, Ts, Ds)
    x = _layernorm(x + _L0_attn_ref(x, L0_attn_Wq, L0_attn_bq, L0_attn_Wk, L0_attn_bk, L0_attn_Wv, L0_attn_bv, L0_attn_Wo, L0_attn_bo, L0_attn_m), axis=-1)
    x = _layernorm(x + _L0_xattn_ref(x, ctx_1024, ctx_1024, L0_xattn_Wq, L0_xattn_bq, L0_xattn_Wk, L0_xattn_bk, L0_xattn_Wv, L0_xattn_bv, L0_xattn_Wo, L0_xattn_bo), axis=-1)
    x = _layernorm(x + _L0_ffn_ref(x, L0_ffn_gate_w, L0_ffn_gate_b, L0_ffn_w1, L0_ffn_b1, L0_ffn_w2, L0_ffn_b2), axis=-1)
    x = _layernorm(x + _L1_attn_ref(x, L1_attn_Wq, L1_attn_bq, L1_attn_Wk, L1_attn_bk, L1_attn_Wv, L1_attn_bv, L1_attn_Wo, L1_attn_bo, L1_attn_Wc), axis=-1)
    x = _layernorm(x + _L1_xattn_ref(x, ctx_1024, ctx_1024, L1_xattn_Wq, L1_xattn_bq, L1_xattn_Wk, L1_xattn_bk, L1_xattn_Wv, L1_xattn_bv, L1_xattn_Wo, L1_xattn_bo), axis=-1)
    x = _layernorm(x + _L1_ffn_ref(x, L1_ffn_Wg, L1_ffn_ln_scale, L1_ffn_ln_bias, L1_ffn_W1, L1_ffn_b1, L1_ffn_W2, L1_ffn_b2), axis=-1)
    return x

_drawn_inputs = setup_inputs


def setup_inputs(seed=0):
    import zlib

    import numpy as np

    out = dict(_drawn_inputs(seed))
    spreads = {'L0_attn_bq': (0.0, 0.663),
     'L0_attn_bk': (0.0, 0.457),
     'L0_attn_bv': (0.0, 0.463),
     'L0_attn_bo': (0.0, 0.1),
     'L0_attn_m': (0.5, 0.6),
     'L0_xattn_bq': (0.0, 0.28),
     'L0_xattn_bk': (0.0, 0.8),
     'L0_xattn_bv': (0.0, 0.1),
     'L0_xattn_bo': (0.0, 0.1),
     'L0_ffn_gate_b': (0.0, 0.8),
     'L0_ffn_b1': (0.0, 0.8),
     'L0_ffn_b2': (0.0, 0.8),
     'L1_attn_bq': (0.0, 0.399),
     'L1_attn_bk': (0.0, 0.8),
     'L1_attn_bv': (0.0, 0.1),
     'L1_attn_bo': (0.0, 0.1),
     'L1_xattn_bq': (0.0, 0.318),
     'L1_xattn_bk': (0.0, 0.8),
     'L1_xattn_bv': (0.0, 0.1),
     'L1_xattn_bo': (0.0, 0.1),
     'L1_ffn_ln_scale': (1.0, 0.6),
     'L1_ffn_ln_bias': (0.0, 0.8),
     'L1_ffn_b1': (0.0, 0.8),
     'L1_ffn_b2': (0.0, 0.1)}
    factors = {'L0_attn_Wq': 3.046,
     'L0_attn_Wk': 4.119,
     'L0_attn_Wv': 4.14,
     'L0_attn_Wo': 2.951,
     'L0_ffn_gate_w': 8.0,
     'L0_ffn_w1': 8.0,
     'L0_ffn_w2': 8.0,
     'L1_ffn_W1': 4.182,
     'L1_ffn_W2': 3.877}
    for name, (base, spread) in spreads.items():
        noise = np.random.default_rng([zlib.crc32(name.encode()), seed]).standard_normal(out[name].shape)
        drawn = base * np.exp(spread * noise) if base else spread * noise
        out[name] = jnp.asarray(drawn.astype(out[name].dtype))
    for name, factor in factors.items():
        out[name] = (out[name] * factor).astype(out[name].dtype)
    return out
```

```python
import math
from contextlib import ExitStack

import concourse.bass as bass
from concourse import mybir
from concourse.alu_op_type import AluOpType as ALU

ACT = mybir.ActivationFunctionType
AX = mybir.AxisListType
F32 = mybir.dt.float32
F16 = mybir.dt.float16
BF16 = mybir.dt.bfloat16
U32 = mybir.dt.uint32

B, S, D = 128, 64, 128
H, HD = 16, 8
P = 128
TILES = B * S // P
T = 8
GROUPS = TILES // T
GT = T * P
HALF = T // 2
NEG = -1.0e30
LN_EPS = 1e-5
NORM_EPS = 1e-12
LN_S = math.log(S)
DMA = 16


def next_group(i, u):
    return (i, 1) if u == 0 else (i + 1, 0)


def prev_group(i, u):
    return (i - 1, 1) if u == 0 else (i, 0)


def positive(v):
    return not isinstance(v, int) or v > 0


def is_last(n):
    return isinstance(n, int) and n == GROUPS - 1


def run_groups(eng, group):
    group(0, 0)
    group(0, 1)
    with eng.Fori(1, GROUPS // 2 - 1) as i:
        for u in range(2):
            group(i, u)
    group(GROUPS // 2 - 1, 0)
    group(GROUPS // 2 - 1, 1)


def tiles_of(dram, g):
    return dram[bass.ds(g * GT, GT), :].rearrange("(t p) d -> p t d", p=P)


class Semaphores:

    def __init__(self, nc, tag):
        self.nc, self.tag, self.all = nc, tag, []

    def __enter__(self):
        return self

    def __call__(self, name):
        self.all.append(self.nc.alloc_semaphore(f"{self.tag}_{name}"))
        return self.all[-1]

    def __exit__(self, *error):
        if error[0] is None:
            self.nc.clear_and_free_semaphores(self.all)
            self.nc.all_engine_barrier()


class Constants:

    def __init__(self, nc, ctx):
        def sb(name, shape, dt):
            return ctx.enter_context(nc.sbuf_tensor(name, shape, dt))

        self.ident = sb("ident", [P, P], F32)
        self.ident_b = sb("ident_b", [P, P], BF16)
        self.causal = sb("causal", [P, 8, S], BF16)
        self.neg_own = sb("neg_own", [P, 32, 32], BF16)
        self.of_own = sb("of_own", [P, P], BF16)
        self.ones_row = sb("ones_row", [1, P], F32)
        self.q_st = sb("q_st", [P, 2, 4, 4, GT], F16)
        self.k_st = sb("k_st", [P, 2, 4, GT], F16)


def make_constants(nc, c):
    with ExitStack() as ctx:
        sem = ctx.enter_context(Semaphores(nc, "constants"))
        filled, selected = sem("filled"), sem("selected")
        block = ctx.enter_context(nc.Block())

        @block.vector
        def _(dve):
            nc.vector.memset(c.ident[:, :], 0.0).then_inc(filled, 1)
            nc.vector.memset(c.ident_b[:, :], 0.0).then_inc(filled, 1)
            nc.vector.memset(c.causal[:, :, :], 0.0).then_inc(filled, 1)
            nc.vector.memset(c.neg_own[:, :, :], 0.0).then_inc(filled, 1)
            nc.vector.memset(c.of_own[:, :], 0.0).then_inc(filled, 1)
            nc.vector.memset(c.ones_row[:, :], 1.0).then_inc(filled, 1)
            dve.wait_ge(filled, 6)
            for b in range(2):
                rows = slice(64 * b, 64 * b + 64)
                nc.vector.memset(c.of_own[32 * b:32 * b + 32, rows], 1.0).then_inc(filled, 1)

        @block.gpsimd
        def _(pool):
            pool.wait_ge(filled, 6)
            done = 0
            for m in (c.ident, c.ident_b):
                pool.wait_ge(selected, done)
                done += 1
                nc.gpsimd.affine_select(out=m[:, :], in_=m[:, :], compare_op=ALU.not_equal, fill=1.0, base=0,
                                        pattern=[[-1, P]], channel_multiplier=1).then_inc(selected, 1)
            for b in range(2):
                m = c.causal[64 * b:64 * b + 64, :, :]
                pool.wait_ge(selected, done)
                done += 1
                nc.gpsimd.affine_select(out=m, in_=m, compare_op=ALU.is_ge, fill=NEG, base=0,
                                        pattern=[[0, 8], [1, S]], channel_multiplier=-1).then_inc(selected, 1)
            for r in range(4):
                m = c.neg_own[32 * r:32 * r + 32, :, :]
                pool.wait_ge(selected, done)
                done += 1
                nc.gpsimd.affine_select(out=m, in_=m, compare_op=ALU.not_equal, fill=-1.0, base=0,
                                        pattern=[[-1, 32], [0, 32]], channel_multiplier=1).then_inc(selected, 1)
            pool.wait_ge(selected, 8)


class Turn:

    def __init__(self, i, k, per=2):
        self.base, self.k, self.per = i, k, per
        self.u, self.i, self.n = k % 2, per // 2 * i + k // 2, per * i + k
        self.v, self.j = k % per, i + k // per

    def after(self, d):
        return Turn(self.base, self.k + d, self.per)

    def live(self, count):
        return not isinstance(self.n, int) or 0 <= self.n < count

    def from_(self, least):
        return not isinstance(self.n, int) or self.n >= least


def quarter_tiles(dram, n):
    return dram[bass.ds(n * HALF * P, HALF * P), :].rearrange("(t p) d -> p t d", p=P)


def cross_attention(nc, c, tag, x_in, ctx_in, x_out, w, causal):
    with ExitStack() as ctx:
        def sb(name, shape, dt=F32):
            return ctx.enter_context(nc.sbuf_tensor(f"{tag}_{name}", shape, dt))

        def ps(name, shape):
            return ctx.enter_context(nc.psum_tensor(f"{tag}_{name}", shape, F32))

        sem = ctx.enter_context(Semaphores(nc, tag))

        def sem2(name):
            return [sem(f"{name}{u}") for u in range(2)]

        wq, wk, wv, wo = (sb(n, [P, P]) for n in ("wq", "wk", "wv", "wo"))
        wq_p, wk_p = sb("wq_p", [P, P]), sb("wk_p", [P, P])
        wo_p = sb("wo_p", [P, P])
        rows = sb("rows", [1, 4, P])
        rows_p = sb("rows_p", [1, 2, P])
        bcol = sb("bcol", [P, 2])
        bv_w = sb("bv_w", [P, P])
        bo_all = sb("bo_all", [P, P])
        x_sb = sb("x", [P, 2, T, P])
        c_sb = sb("c", [P, 2, T, P])
        xT = sb("xT", [P, GT])
        cT = sb("cT", [P, GT])
        q_hi, q_lo, k_hi, k_lo = (sb(n, [P, GT], F16) for n in ("q_hi", "q_lo", "k_hi", "k_lo"))
        q_st, k_st = c.q_st, c.k_st
        v_st = sb("v_st", [P, 2, T, H, 32])
        prob = sb("prob", [P, 2, H * S])
        mt = sb("mt", [P, 32])
        mc = sb("mc", [64, 32], BF16)
        lower = sb("lower", [P, 2, 32, 32], BF16)
        av = sb("av", [P, 2, 4, T * S])
        sums = sb("sums", [P, 2, S])
        num, rec = sb("num", [P, 2, T * S]), sb("rec", [P, 2, T * S])
        rec_dram = nc.dram_tensor(f"{tag}_recs", [H, 2, T, S], F32, kind="Internal").ap()
        o_n = sb("o_n", [P, T, 2, S])
        x_res = sb("x_res", [P, T, P])
        y = sb("y", [P, T, P])
        stats = sb("stats", [P, T, 6])
        mv = sb("mv", [P, T, 2])
        var_eps, rstd, neg_half = sb("var_eps", [P, T]), sb("rstd", [P, T]), sb("neg_half", [P, T])

        score = [ps(f"score{t}", [P, 2, 512]) for t in range(2)]
        proj = [ps(f"proj{h}", [P, 512]) for h in range(2)]
        av_ps = ps("av_ps", [P, 4, S])
        mt_ps = ps("mt_ps", [64, 64])

        w_loaded, w_ready, w_cols, b_ready = sem("w_loaded"), sem("w_ready"), sem("w_cols"), sem("b_ready")
        cleared, cleared1 = sem("cleared"), sem("cleared1")
        x_loaded, c_loaded, q_placed, k_placed, o_placed = map(
            sem2, ("x_loaded", "c_loaded", "q_placed", "k_placed", "o_placed"))
        res_loaded, stored = sem("res_loaded"), sem("stored")
        xT_ps, cT_ps, q_ps, k_ps, v_ps, o_ps = map(sem, ("xT_ps", "cT_ps", "q_ps", "k_ps", "v_ps", "o_ps"))
        s_done, mt_done, low_done, av_done = map(sem, ("s_done", "mt_done", "low_done", "av_done"))
        xT_sb, cT_sb, q_hi_ok, k_hi_ok, v_sb, exp_done, av_sb = map(
            sem, ("xT_sb", "cT_sb", "q_hi_ok", "k_hi_ok", "v_sb", "exp_done", "av_sb"))
        q_lo_ok, k_lo_ok, max_done, mc_done, lower_done = map(
            sem, ("q_lo_ok", "k_lo_ok", "max_done", "mc_done", "lower_done"))
        recs_out, recs_in, recip_done, normed, res_done, stat_done, mv_done = map(
            sem, ("recs_out", "recs_in", "recip_done", "normed", "res_done", "stat_done", "mv_done"))
        res_biased, eps_done, rstd_done, ln_done = map(sem, ("res_biased", "eps_done", "rstd_done", "ln_done"))

        passed = sem("passed")

        QPLACE, KPLACE = 12, 3
        OPLACE = 4
        PARTS = ((q_hi, q_lo, q_hi), (k_hi, k_hi, k_lo))

        def load(n, u):
            nc.sync.dma_start(x_sb[:, u, :, :], tiles_of(x_in, n)).then_inc(x_loaded[u], DMA)
            nc.sync.dma_start(c_sb[:, u, :, :], tiles_of(ctx_in, n)).then_inc(c_loaded[u], DMA)

        with nc.Block() as block:
            @block.sync
            def _(sp):
                for dst, name in ((wq, "Wq"), (wk, "Wk"), (wv, "Wv"), (wo, "Wo")):
                    sp.dma_start(dst[:, :], w[name]).then_inc(w_loaded, DMA)
                for n, name in enumerate(("bq", "bk", "bv", "bo")):
                    sp.dma_start(rows[0:1, n, :], w[name].rearrange("(a d) -> a d", a=1)).then_inc(w_loaded, DMA)
                for qd in range(4):
                    src = w["Wo"][32 * qd:32 * qd + 32, :].rearrange("(j d) o -> d j o", d=HD)
                    sp.dma_start(wo_p[32 * qd:32 * qd + 32, :], src).then_inc(w_loaded, DMA)
                for u in range(2):
                    load(u, u)
                sp.wait_ge(w_loaded, 12 * DMA)

            @block.vector
            def _(dve):
                nc.vector.memset(v_st[:, 0, :, :, :], 0.0).then_inc(cleared, 1)
                nc.vector.memset(neg_half[:, :], -0.5).then_inc(cleared, 1)
                nc.vector.memset(lower[:, :, :, :], 0.0).then_inc(cleared, 1)
                dve.wait_ge(cleared, 1)
                for b in range(2):
                    nc.vector.memset(v_st[64 * b:64 * b + 64, 0, :, :, :].rearrange("p t h c -> p (t h) c")
                                     [:, :, 2 + b:32:4], 1.0).then_inc(cleared, 1)
                dve.wait_ge(w_loaded, 12 * DMA)
                scale = float(HD) ** -0.5
                perm = "k (f h d) -> k h d f"
                nc.vector.tensor_scalar(wq_p[:, :].rearrange("k (h d f) -> k h d f", h=4, f=4),
                                        wq[:, :].rearrange(perm, h=4, f=4), scale, None, ALU.mult).then_inc(w_ready, 1)
                nc.vector.tensor_copy(wk_p[:, :].rearrange("k (h d f) -> k h d f", h=4, f=4),
                                      wk[:, :].rearrange(perm, h=4, f=4)).then_inc(w_ready, 1)
                for n, f in ((0, scale), (1, 1.0)):
                    nc.vector.tensor_scalar(rows_p[0:1, n, :].rearrange("k (h d f) -> k h d f", h=4, f=4),
                                            rows[0:1, n, :].rearrange(perm, h=4, f=4), f, None, ALU.mult)\
                      .then_inc(w_ready, 1)
                dve.wait_ge(w_cols, 1)
                nc.vector.tensor_copy(bcol[:, :], proj[0][:, 0:2]).then_inc(b_ready, 1)
                nc.vector.tensor_copy(bv_w[:, :], proj[0][:, 128:256]).then_inc(b_ready, 1)
                dve.wait_ge(w_cols, 2)
                nc.vector.tensor_copy(bo_all[:, :], proj[1][:, 0:128]).then_inc(b_ready, 1)

            @block.gpsimd
            def _(pool):
                nc.gpsimd.memset(v_st[:, 1, :, :, :], 0.0).then_inc(cleared1, 1)
                for b in range(2):
                    pool.wait_ge(cleared1, b + 1)
                    nc.gpsimd.memset(v_st[64 * b:64 * b + 64, 1, :, :, :].rearrange("p t h c -> p (t h) c")
                                     [:, :, 2 + b:32:4], 1.0).then_inc(cleared1, 1)

            @block.tensor
            def _(pe):
                pe.wait_ge(w_ready, 4)
                for n in range(2):
                    nc.tensor.matmul(proj[0][:, n:n + 1], rows_p[0:1, n, :], c.ones_row[0:1, 0:1], start=True, stop=True)
                nc.tensor.matmul(proj[0][:, 128:256], rows[0:1, 2, :], c.ones_row[0:1, :],
                                 start=True, stop=True).then_inc(w_cols, 1)
                pe.wait_ge(b_ready, 2)
                nc.tensor.matmul(proj[1][:, 0:128], bv_w[:, :], wo[:, :], start=True, stop=False)
                nc.tensor.matmul(proj[1][:, 0:128], c.ones_row[0:1, :], rows[0:1, 3, :],
                                 start=False, stop=True).then_inc(w_cols, 1)

        block = ctx.enter_context(nc.Block())

        @block.sync
        def _(sp):
            def place_q(n, i, u):
                sp.wait_ge(q_lo_ok, 2 * n + 2)
                sp.sem_inc(passed, 1)
                if not (isinstance(n, int) and n < 2):
                    sp.wait_ge(s_done, T * (n - 1))
                for h4 in range(4):
                    for part, src in enumerate(PARTS[0]):
                        r = 32 * part + 8 * h4
                        sp.dma_start(q_st[r:r + 8, u, :, h4, :], src[32 * h4:32 * h4 + 32, :])\
                          .then_inc(q_placed[u], DMA)

            def place_k(n, i, u):
                sp.wait_ge(k_lo_ok, 2 * n + 2)
                sp.sem_inc(passed, 1)
                if positive(n - 1):
                    sp.wait_ge(s_done, T * (n - 1))
                for part, src in enumerate(PARTS[1]):
                    sp.dma_start(k_st[32 * part:32 * part + 32, u, :, :], src[:, :]).then_inc(k_placed[u], DMA)

            def place_o(n, i, u):
                sp.wait_ge(av_sb, T * n + T)
                sp.sem_inc(passed, 1)
                if positive(n):
                    sp.wait_ge(normed, n)
                    sp.sem_inc(passed, 1)
                if positive(n):
                    sp.wait_ge(recs_out, 2 * DMA * n)
                    sp.sem_inc(passed, 1)
                for b in range(2):
                    sp.dma_start(sums[:, b, :], av[2 + b:P:32, u, :, :]).then_inc(o_placed[u], DMA)
                for b in range(2):
                    sp.dma_start(num[:, b, :], av[b:P:4, u, :, :]).then_inc(o_placed[u], DMA)

            def spread_recs(n):
                sp.wait_ge(recip_done, n + 1)
                sp.sem_inc(passed, 1)
                if positive(n):
                    sp.wait_ge(recs_in, 4 * DMA * n)
                    sp.sem_inc(passed, 1)
                for b in range(2):
                    sp.dma_start(rec_dram[:, b, :, :], sums[:, b, :]).then_inc(recs_out, DMA)
                sp.wait_ge(recs_out, 2 * DMA * (n + 1))
                sp.sem_inc(passed, 1)
                for qd in range(4):
                    src = rec_dram[4 * qd:4 * qd + 4, :, :, :].rearrange("j b t q -> (j b t q)")
                    sp.dma_start(rec[32 * qd:32 * qd + 32, :, :], src.unsqueeze(0).to_broadcast([HD, 4 * 2 * T * S]))\
                      .then_inc(recs_in, DMA)

            def load_residual(n):
                if positive(n):
                    sp.wait_ge(res_done, 2 * n)
                sp.sem_inc(passed, 1)
                sp.dma_start(x_res[:, :, :], tiles_of(x_in, n)).then_inc(res_loaded, DMA)

            def store(n):
                sp.wait_ge(ln_done, T * n + T)
                sp.sem_inc(passed, 1)
                sp.dma_start(tiles_of(x_out, n), y[:, :, :]).then_inc(stored, DMA)

            def group(i, u):
                n = 2 * i + u
                if positive(n):
                    load_residual(n - 1)
                    place_o(n - 1, *prev_group(i, u))
                if positive(n):
                    spread_recs(n - 1)
                if positive(n - 1):
                    store(n - 2)
                if not is_last(n):
                    place_q(n + 1, *next_group(i, u))
                    place_k(n + 1, *next_group(i, u))
                if not (isinstance(n, int) and n >= GROUPS - 2):
                    sp.wait_ge(cT_ps, 2 * n + 4)
                    sp.sem_inc(passed, 1)
                    load(n + 2, u)

            place_q(0, 0, 0)
            place_k(0, 0, 0)
            run_groups(sp, group)
            load_residual(GROUPS - 1)
            place_o(GROUPS - 1, GROUPS // 2 - 1, 1)
            spread_recs(GROUPS - 1)
            for n in (GROUPS - 2, GROUPS - 1):
                store(n)
            sp.wait_ge(stored, DMA * GROUPS)

        @block.gpsimd
        def _(pool):
            def bias_residual(n):
                pool.wait_ge(res_loaded, DMA * n + DMA)
                nc.gpsimd.tensor_tensor(x_res[:, :, :], x_res[:, :, :],
                                        bo_all[:, :].unsqueeze(1).to_broadcast([P, T, P]), ALU.add)\
                  .then_inc(res_biased, 1)

            def deviations(n):
                pool.wait_ge(mv_done, n + 1)
                pool.sem_inc(passed, 1)
                nc.gpsimd.tensor_scalar(var_eps[:, :], mv[:, :, 1], LN_EPS, None, ALU.add).then_inc(eps_done, 1)
                pool.wait_ge(eps_done, n + 1)
                nc.gpsimd.tensor_tensor(rstd[:, :], var_eps[:, :], neg_half[:, :], ALU.pow).then_inc(rstd_done, 1)

            def normalise(n):
                pool.wait_ge(rstd_done, n + 1)
                pool.sem_inc(passed, 1)
                for t in range(T):
                    nc.gpsimd.tensor_scalar(y[:, t, :], y[:, t, :], mv[:, t, 0:1], rstd[:, t:t + 1],
                                            ALU.subtract, ALU.mult).then_inc(ln_done, 1)

            def group(i, u):
                n = 2 * i + u
                if positive(n - 1):
                    deviations(n - 2)
                    normalise(n - 2)
                if positive(n):
                    bias_residual(n - 1)

            run_groups(pool, group)
            deviations(GROUPS - 2)
            bias_residual(GROUPS - 1)
            normalise(GROUPS - 2)
            deviations(GROUPS - 1)

        X_T, Q, C_T, K, V, NONE, OUT = range(T - 1)

        @block.scalar
        def _(act):
            def evacuate(n, i, u, r, h):
                cols = slice(512 * h, 512 * h + 512)
                if r == X_T:
                    act.wait_ge(xT_ps, 2 * n + h + 1)
                    nc.scalar.activation(xT[:, cols], proj[h][:, :], ACT.Copy).then_inc(xT_sb, 1)
                elif r == Q:
                    act.wait_ge(q_ps, 2 * n + h + 1)
                    if h == 0 and positive(n):
                        pi, pu = prev_group(i, u)
                        act.wait_ge(q_placed[pu], DMA * QPLACE * (pi + 1))
                    nc.scalar.activation(q_hi[:, cols], proj[h][:, :], ACT.Identity, bias=bcol[:, 0:1]).then_inc(q_hi_ok, 1)
                elif r == C_T:
                    act.wait_ge(cT_ps, 2 * n + h + 1)
                    nc.scalar.activation(cT[:, cols], proj[h][:, :], ACT.Copy).then_inc(cT_sb, 1)
                elif r == K:
                    act.wait_ge(k_ps, 2 * n + h + 1)
                    if h == 0 and positive(n):
                        pi, pu = prev_group(i, u)
                        act.wait_ge(k_placed[pu], DMA * KPLACE * (pi + 1))
                    nc.scalar.activation(k_hi[:, cols], proj[h][:, :], ACT.Identity, bias=bcol[:, 1:2]).then_inc(k_hi_ok, 1)
                elif r == V:
                    act.wait_ge(v_ps, 2 * n + h + 1)
                    for b in range(2):
                        rows_b = slice(64 * b, 64 * b + 64)
                        nc.scalar.activation(v_st[rows_b, u, HALF * h:HALF * h + HALF, :, b:32:4],
                                             proj[h][rows_b, :].rearrange("p (t h d) -> p t h d", h=H, d=HD),
                                             ACT.Copy).then_inc(v_sb, 1)

            def exp(t, t2):
                act.wait_ge(low_done, t + 1)
                if positive(t - 1):
                    act.wait_ge(av_done, t - 1)
                nc.scalar.activation(prob[:, t2, :], score[t2][:, :, :].rearrange("p a c -> p (a c)"), ACT.Exp)\
                  .then_inc(exp_done, 1)

            def copy_av(t, r, i, u):
                act.wait_ge(av_done, t + 1)
                if r == 0 and positive(i):
                    act.wait_ge(o_placed[u], DMA * OPLACE * i)
                nc.scalar.activation(av[:, u, :, S * r:S * r + S], av_ps[:, :, :], ACT.Copy).then_inc(av_sb, 1)

            def group(i, u):
                n = 2 * i + u
                pi, pu = prev_group(i, u)
                ni, nu = next_group(i, u)
                for r in range(T):
                    t = T * n + r
                    prepares = r <= V and not is_last(n)
                    if prepares:
                        evacuate(n + 1, ni, nu, r, 0)
                    if r > 0:
                        copy_av(t - 1, r - 1, i, u)
                    elif positive(n):
                        copy_av(t - 1, T - 1, pi, pu)
                    exp(t, r % 2)
                    if prepares:
                        evacuate(n + 1, ni, nu, r, 1)

            for r in (X_T, Q, C_T, K, V):
                for h in range(2):
                    evacuate(0, 0, 0, r, h)
            run_groups(act, group)
            copy_av(TILES - 1, T - 1, GROUPS // 2 - 1, 1)

        @block.vector
        def _(dve):
            def low_part(n, r, h):
                cols = slice(512 * h, 512 * h + 512)
                hi, lo, hi_ok, lo_ok, col = (q_hi, q_lo, q_hi_ok, q_lo_ok, 0) if r == Q else (k_hi, k_lo, k_hi_ok, k_lo_ok, 1)
                dve.wait_ge(hi_ok, 2 * n + h + 1)
                nc.vector.scalar_tensor_tensor(out=lo[:, cols], in0=proj[h][:, :], scalar=bcol[:, col:col + 1],
                                               in1=hi[:, cols], op0=ALU.add, op1=ALU.subtract).then_inc(lo_ok, 1)

            def row_max(t, t2):
                dve.wait_ge(s_done, t + 1)
                nc.vector.tensor_reduce(mt[:, :], score[t2][:, :, :].rearrange("p a (c q) -> p (a c) q", q=32),
                                        AX.X, ALU.max, apply_transpose=True).then_inc(max_done, 1)

            def spread_max(t, t2):
                dve.wait_ge(mt_done, t + 1)
                if positive(t):
                    dve.wait_ge(lower_done, t)
                nc.vector.tensor_reduce(mc[:, :], mt_ps[:, :].rearrange("p (k q) -> p q k", k=2), AX.X, ALU.max)\
                  .then_inc(mc_done, 1)
                dve.wait_ge(mc_done, t + 1)
                nc.vector.tensor_tensor(lower[0:64, t2, :, :], mc[:, :].unsqueeze(1).to_broadcast([64, 32, 32]),
                                        c.neg_own[0:64, :, :], ALU.mult).then_inc(lower_done, 1)

            def reciprocals(n, i, u):
                dve.wait_ge(o_placed[u], DMA * OPLACE * (i + 1))
                nc.vector.reciprocal(sums[:, :, :], sums[:, :, :]).then_inc(recip_done, 1)

            def divide(n):
                dve.wait_ge(recs_in, 4 * DMA * (n + 1))
                if positive(n):
                    dve.wait_ge(o_ps, 2 * n)
                nc.vector.tensor_tensor(o_n[:, :, :, :].rearrange("p t b q -> p b t q"),
                                        num[:, :, :].rearrange("p b (t q) -> p b t q", q=S),
                                        rec[:, :, :].rearrange("p b (t q) -> p b t q", q=S), ALU.mult)\
                  .then_inc(normed, 1)

            def residual(n, h):
                dve.wait_ge(o_ps, 2 * n + h + 1)
                if h == 0:
                    dve.wait_ge(res_biased, n + 1)
                    dve.wait_ge(stored, DMA * n)
                nc.vector.tensor_tensor(y[:, HALF * h:HALF * h + HALF, :],
                                        proj[h][:, :].rearrange("p (t d) -> p t d", d=P),
                                        x_res[:, HALF * h:HALF * h + HALF, :], ALU.add).then_inc(res_done, 1)

            def half_stats(n, h):
                dve.wait_ge(res_done, 2 * n + h + 1)
                for t in range(HALF * h, HALF * h + HALF):
                    nc.vector.bn_stats(stats[:, t, :], y[:, t, :]).then_inc(stat_done, 1)

            def moments(n):
                dve.wait_ge(stat_done, T * n + T)
                dve.sem_inc(passed, 1)
                for t in range(T):
                    ins = nc.vector.bn_aggr(mv[:, t, :], stats[:, t, :])
                ins.then_inc(mv_done, 1)

            def group(i, u):
                n = 2 * i + u
                for r in range(T):
                    t = T * n + r
                    spread_max(t, r % 2)
                    if not is_last(n):
                        if r in (Q, K):
                            low_part(n + 1, r, 0)
                        elif r - 1 in (Q, K):
                            low_part(n + 1, r - 1, 1)
                    if positive(n):
                        if r == 2:
                            reciprocals(n - 1, *prev_group(i, u))
                        elif r == V + 1:
                            divide(n - 1)
                        elif r in (OUT, OUT + 1):
                            residual(n - 1, r - OUT)
                            half_stats(n - 1, r - OUT)
                    if not (is_last(n) and r == T - 1):
                        row_max(t + 1, (r + 1) % 2)
                    if positive(n) and r == OUT + 1:
                        moments(n - 1)

            for r in (Q, K):
                for h in range(2):
                    low_part(0, r, h)
            row_max(0, 0)
            run_groups(dve, group)
            reciprocals(GROUPS - 1, GROUPS // 2 - 1, 1)
            divide(GROUPS - 1)
            for h in range(2):
                residual(GROUPS - 1, h)
                half_stats(GROUPS - 1, h)
            moments(GROUPS - 1)
            dve.wait_ge(rstd_done, GROUPS)
            for t in range(T):
                nc.vector.tensor_scalar(y[:, t, :], y[:, t, :], mv[:, t, 0:1], rstd[:, t:t + 1],
                                        ALU.subtract, ALU.mult).then_inc(ln_done, 1)

        @block.tensor
        def _(pe):
            def prepare(n, i, u, r, h):
                out = proj[h]
                if r == X_T:
                    pe.wait_ge(x_loaded[u], DMA * (i + 1))
                    if positive(n):
                        pe.wait_ge(v_sb, 4 * n - 2 + 2 * h)
                    if positive(n - 2):
                        pe.wait_ge(res_done, 2 * (n - 3) + h + 1)
                    for t in range(HALF):
                        ins = nc.tensor.transpose(out[:, P * t:P * t + P], x_sb[:, u, HALF * h + t, :], c.ident[:, :])
                    ins.then_inc(xT_ps, 1)
                elif r == Q:
                    pe.wait_ge(xT_sb, 2 * n + h + 1)
                    nc.tensor.matmul(out[:, :], wq_p[:, :], xT[:, 512 * h:512 * h + 512], start=True, stop=True)\
                      .then_inc(q_ps, 1)
                elif r == C_T:
                    pe.wait_ge(c_loaded[u], DMA * (i + 1))
                    pe.wait_ge(q_lo_ok, 2 * n + h + 1)
                    for t in range(HALF):
                        ins = nc.tensor.transpose(out[:, P * t:P * t + P], c_sb[:, u, HALF * h + t, :], c.ident[:, :])
                    ins.then_inc(cT_ps, 1)
                elif r == K:
                    pe.wait_ge(cT_sb, 2 * n + h + 1)
                    nc.tensor.matmul(out[:, :], wk_p[:, :], cT[:, 512 * h:512 * h + 512], start=True, stop=True)\
                      .then_inc(k_ps, 1)
                elif r == V:
                    pe.wait_ge(k_lo_ok, 2 * n + h + 1)
                    for t in range(HALF):
                        ins = nc.tensor.matmul(out[:, P * t:P * t + P], cT[:, P * (HALF * h + t):P * (HALF * h + t + 1)],
                                               wv[:, :], start=True, stop=True)
                    ins.then_inc(v_ps, 1)

            def project_o(n, h, after_v):
                pe.wait_ge(normed, n + 1)
                if after_v:
                    pe.wait_ge(v_sb, 4 * (n + 2) + 2 * h + 2)
                else:
                    pe.wait_ge(res_done, 2 * (n - 1) + h + 1)
                for t in range(HALF):
                    ins = nc.tensor.matmul(proj[h][:, P * t:P * t + P],
                                           o_n[:, HALF * h + t, :, :].rearrange("p b q -> p (b q)"), wo_p[:, :],
                                           start=True, stop=True)
                ins.then_inc(o_ps, 1)

            def scores(t, r, i, u):
                if r == 0:
                    pe.wait_ge(q_placed[u], DMA * QPLACE * (i + 1))
                    pe.wait_ge(k_placed[u], DMA * KPLACE * (i + 1))
                if positive(t - 1):
                    pe.wait_ge(exp_done, t - 1)
                s = score[r % 2]
                if causal:
                    for half in range(2):
                        nc.tensor.matmul(s[:, half, :], c.ident_b[:, :], c.causal[:, :, :].rearrange("p h q -> p (h q)"),
                                         start=True, stop=False, skip_group_check=True)
                for f in range(4):
                    for b in range(2):
                        tok = slice(P * r + S * b, P * r + S * b + S)
                        ins = nc.tensor.matmul(s[64 * b:64 * b + 64, f // 2, 256 * (f % 2):256 * (f % 2) + 256],
                                               k_st[:, u, f, tok], q_st[:, u, f, :, tok],
                                               start=(not causal and f % 2 == 0), stop=False, skip_group_check=True)
                ins.then_inc(s_done, 1)

            def transpose_max(t):
                pe.wait_ge(max_done, t + 1)
                for b in range(2):
                    ins = nc.tensor.matmul(mt_ps[32 * b:32 * b + 32, :], mt[:, :], c.ident[:, 64 * b:64 * b + 64],
                                           start=True, stop=True)
                ins.then_inc(mt_done, 1)

            def lower_scores(t, t2):
                pe.wait_ge(lower_done, t + 1)
                for half in range(2):
                    ins = nc.tensor.matmul(score[t2][:, half, :], c.of_own[:, :],
                                           lower[:, t2, 16 * half:16 * half + 16, :].rearrange("p a q -> p (a q)"),
                                           start=False, stop=True, skip_group_check=True)
                ins.then_inc(low_done, 1)

            def values(t, r, n, u):
                pe.wait_ge(exp_done, t + 1)
                if positive(t):
                    pe.wait_ge(av_sb, t)
                if r == 0:
                    pe.wait_ge(v_sb, 4 * n + 4)
                for j in range(4):
                    for qd in range(4):
                        h = 4 * qd + j
                        ins = nc.tensor.matmul(av_ps[32 * qd:32 * qd + 32, j, :], v_st[:, u, r, h, :],
                                               prob[:, r % 2, S * h:S * h + S], start=True, stop=True)
                ins.then_inc(av_done, 1)

            def group(i, u):
                n = 2 * i + u
                pi, pu = prev_group(i, u)
                ni, nu = next_group(i, u)
                for r in range(T):
                    t = T * n + r
                    for h in range(2):
                        if h == 0:
                            transpose_max(t)
                        if r <= V and not is_last(n):
                            prepare(n + 1, ni, nu, r, h)
                        if r == OUT and positive(n):
                            project_o(n - 1, h, after_v=not is_last(n))
                        if h == 0:
                            if r > 0:
                                values(t - 1, r - 1, n, u)
                            elif positive(n):
                                values(t - 1, T - 1, n - 1, pu)
                            if r < T - 1:
                                scores(t + 1, r + 1, i, u)
                            elif not is_last(n):
                                scores(t + 1, 0, ni, nu)
                            lower_scores(t, r % 2)

            for r in (X_T, Q, C_T, K, V):
                for h in range(2):
                    prepare(0, 0, 0, r, h)
            scores(0, 0, 0, 0)
            run_groups(pe, group)
            values(TILES - 1, T - 1, GROUPS - 1, 1)
            for h in range(2):
                project_o(GROUPS - 1, h, after_v=False)


def linear_attention(nc, c, tag, x_in, x_out, w):
    STEPS = TILES // HALF
    with ExitStack() as ctx:
        def sb(name, shape, dt=F32):
            return ctx.enter_context(nc.sbuf_tensor(f"{tag}_{name}", shape, dt))

        def ps(name, shape):
            return ctx.enter_context(nc.psum_tensor(f"{tag}_{name}", shape, F32))

        sem = ctx.enter_context(Semaphores(nc, tag))

        def sem2(name):
            return [sem(f"{name}{u}") for u in range(2)]

        wqkv = sb("wqkv", [P, 3, P])
        wo = sb("wo", [P, P])
        rows = sb("rows", [1, 4, P])
        m_row, m_wide = sb("m_row", [1, 3, H]), sb("m_wide", [1, H, HD])
        bias = sb("bias", [P, 4, P])
        own_head = sb("own_head", [P, H, HD])
        scale_col = sb("scale_col", [P, 1])
        x_sb = sb("x", [P, 2, HALF, P])
        xT = sb("xT", [P, 2, HALF * P])
        qk = sb("qk", [P, 2, HALF, 2 * P])
        v_z = sb("v_z", [P, 2, 2, HALF, P])
        sq = sb("sq", [P, HALF * 2 * P])
        ss = sb("ss", [P, HALF * 2 * H])
        length = sb("length", [P, HALF * 2 * H])
        inv = sb("inv", [P, 2, HALF * 2 * H])
        qT = sb("qT", [P, 2, HALF * P])
        vk = sb("vk", [P, 2, 2, HALF, P])
        own_w = sb("own_w", [P, 2, HALF, P])
        x_res = sb("x_res", [P, 2, HALF, P])
        y = sb("y", [P, 2, HALF, P])
        stats = sb("stats", [P, HALF, 6])
        mv = sb("mv", [P, HALF, 2])
        var_eps, rstd, neg_half = sb("var_eps", [P, HALF]), sb("rstd", [P, HALF]), sb("neg_half", [P, HALF])

        turned = ps("turned", [P, 512])
        qkv_ps = [ps(f"qkv{u}", [P, 512]) for u in range(2)]
        vk_ps = [ps(f"vk{b}", [P, 512]) for b in range(2)]
        w_ps = [ps(f"w{b}", [P, 512]) for b in range(2)]
        y_ps = ps("y_ps", [P, 512])

        w_loaded, filled, picked, wide, cols, biased = map(
            sem, ("w_loaded", "filled", "picked", "wide", "cols", "biased"))
        x_loaded, res_loaded, stored = map(sem2, ("x_loaded", "res_loaded", "stored"))
        xT_ps, qkv_done, qT_ps, vk_done, w_done, y_done = map(
            sem, ("xT_ps", "qkv_done", "qT_ps", "vk_done", "w_done", "y_done"))
        xT_sb, squared, rooted, qT_sb, w_sb = map(sem, ("xT_sb", "squared", "rooted", "qT_sb", "w_sb"))
        qkv_sb, summed, clamped, inv_done, vk_sb = map(sem, ("qkv_sb", "summed", "clamped", "inv_done", "vk_sb"))
        res_done, stat_done, mv_done = map(sem, ("res_done", "stat_done", "mv_done"))
        unit_done, res_biased, eps_done, rstd_done, ln_done = map(
            sem, ("unit_done", "res_biased", "eps_done", "rstd_done", "ln_done"))
        passed = sem("passed")

        with nc.Block() as block:
            @block.sync
            def _(sp):
                for n, name in enumerate(("Wq", "Wk", "Wv")):
                    sp.dma_start(wqkv[:, n, :], w[name]).then_inc(w_loaded, DMA)
                sp.dma_start(wo[:, :], w["Wo"]).then_inc(w_loaded, DMA)
                for n, name in enumerate(("bq", "bk", "bv", "bo")):
                    sp.dma_start(rows[0:1, n, :], w[name].rearrange("(a d) -> a d", a=1)).then_inc(w_loaded, DMA)
                sp.dma_start(m_row[0:1, 0, :], w["m"].rearrange("(a d) -> a d", a=1)).then_inc(w_loaded, DMA)
                for m in range(2):
                    sp.dma_start(x_sb[:, m, :, :], quarter_tiles(x_in, m)).then_inc(x_loaded[m], DMA)
                sp.wait_ge(w_loaded, 9 * DMA)

            @block.gpsimd
            def _(pool):
                pool.wait_ge(filled, 3)
                nc.gpsimd.affine_select(out=own_head[:, :, :], in_=own_head[:, :, :], compare_op=ALU.is_ge, fill=0.0,
                                        base=0, pattern=[[-HD, H], [0, HD]], channel_multiplier=1).then_inc(picked, 1)
                pool.wait_ge(picked, 1)
                nc.gpsimd.affine_select(out=own_head[:, :, :], in_=own_head[:, :, :], compare_op=ALU.is_ge, fill=0.0,
                                        base=HD - 1, pattern=[[HD, H], [0, HD]], channel_multiplier=-1).then_inc(picked, 1)
                pool.wait_ge(picked, 2)
                nc.gpsimd.memset(c.q_st[:, 1, :, :, :].bitcast(F32), 0.0).then_inc(picked, 1)
                nc.gpsimd.memset(c.k_st[:, :, :, :].bitcast(F32), 0.0).then_inc(picked, 1)

            @block.scalar
            def _(act):
                act.wait_ge(w_loaded, 9 * DMA)
                nc.scalar.activation(m_row[0:1, 1, :], m_row[0:1, 0, :], ACT.Sigmoid).then_inc(wide, 1)
                act.wait_ge(wide, 1)
                nc.scalar.activation(m_row[0:1, 2, :], m_row[0:1, 1, :], ACT.Exp, scale=-LN_S).then_inc(wide, 1)

            @block.vector
            def _(dve):
                nc.vector.memset(own_head[:, :, :], 1.0).then_inc(filled, 1)
                nc.vector.memset(v_z[:, :, :, :, :], 0.0).then_inc(filled, 1)
                nc.vector.memset(neg_half[:, :], -0.5).then_inc(filled, 1)
                nc.vector.memset(c.q_st[:, 0, :, :, :].bitcast(F32), 0.0).then_inc(filled, 1)
                dve.wait_ge(wide, 2)
                nc.vector.tensor_copy(m_wide[0:1, :, :], m_row[0:1, 2, :].unsqueeze(2).to_broadcast([1, H, HD]))\
                  .then_inc(wide, 1)
                dve.wait_ge(cols, 1)
                nc.vector.tensor_copy(scale_col[:, :], y_ps[:, 0:1]).then_inc(biased, 1)
                nc.vector.tensor_copy(bias[:, :, :].rearrange("p n d -> p (n d)"), turned[:, :]).then_inc(biased, 1)
                dve.wait_ge(picked, 2)
                dve.wait_ge(biased, 2)
                nc.vector.tensor_scalar(own_head[:, :, :], own_head[:, :, :], scale_col[:, 0:1], None, ALU.mult)\
                  .then_inc(biased, 1)

            @block.tensor
            def _(pe):
                pe.wait_ge(w_loaded, 9 * DMA)
                pe.wait_ge(wide, 3)
                nc.tensor.matmul(turned[:, :], c.ones_row[0:1, :], rows[0:1, :, :].rearrange("a n d -> a (n d)"),
                                 start=True, stop=True)
                nc.tensor.matmul(y_ps[:, 0:1], m_wide[0:1, :, :].rearrange("a h d -> a (h d)"), c.ones_row[0:1, 0:1],
                                 start=True, stop=True).then_inc(cols, 1)

        block = ctx.enter_context(nc.Block())

        def run(eng, step, ahead=2):
            rounds = (STEPS - ahead) // 2
            for k in range(-2, 2):
                step(Turn(0, k))
            with eng.Fori(1, rounds) as i:
                for u in range(2):
                    step(Turn(i, u))
            for k in range(2 * rounds, STEPS + 2):
                step(Turn(0, k))

        @block.sync
        def _(sp):
            def load_x(m):
                if m.from_(2):
                    sp.wait_ge(xT_ps, m.n - 1)
                    sp.sem_inc(passed, 1)
                    sp.dma_start(x_sb[:, m.u, :, :], quarter_tiles(x_in, m.n)).then_inc(x_loaded[m.u], DMA)

            def load_res(m):
                if m.from_(2):
                    sp.wait_ge(res_done, m.n - 1)
                    sp.sem_inc(passed, 1)
                sp.dma_start(x_res[:, m.u, :, :], quarter_tiles(x_in, m.n)).then_inc(res_loaded[m.u], DMA)

            def store(m):
                sp.wait_ge(ln_done, HALF * (m.n + 1))
                sp.sem_inc(passed, 1)
                sp.dma_start(quarter_tiles(x_out, m.n), y[:, m.u, :, :]).then_inc(stored[m.u], DMA)

            def step(s):
                if s.after(3).live(STEPS):
                    load_x(s.after(3))
                if s.live(STEPS):
                    load_res(s)
                if s.after(-2).live(STEPS):
                    store(s.after(-2))

            run(sp, step, ahead=3)
            for u in range(2):
                sp.wait_ge(stored[u], DMA * STEPS // 2)

        @block.gpsimd
        def _(pool):
            def unit_vectors(m):
                pool.wait_ge(inv_done, m.n + 1)
                nc.gpsimd.tensor_tensor(qk[:, m.u, :, :].rearrange("p t (h d) -> p (t h) d", d=HD),
                                        qk[:, m.u, :, :].rearrange("p t (h d) -> p (t h) d", d=HD),
                                        inv[:, m.u, :].unsqueeze(2).to_broadcast([P, HALF * 2 * H, HD]),
                                        ALU.mult).then_inc(unit_done, 1)

            def bias_residual(m):
                pool.wait_ge(res_loaded[m.u], DMA * (m.i + 1))
                nc.gpsimd.tensor_tensor(x_res[:, m.u, :, :], x_res[:, m.u, :, :],
                                        bias[:, 3, :].unsqueeze(1).to_broadcast([P, HALF, P]), ALU.add)\
                  .then_inc(res_biased, 1)

            def layernorm(m):
                pool.wait_ge(mv_done, m.n + 1)
                pool.sem_inc(passed, 1)
                nc.gpsimd.tensor_scalar(var_eps[:, :], mv[:, :, 1], LN_EPS, None, ALU.add).then_inc(eps_done, 1)
                pool.wait_ge(eps_done, m.n + 1)
                nc.gpsimd.tensor_tensor(rstd[:, :], var_eps[:, :], neg_half[:, :], ALU.pow).then_inc(rstd_done, 1)
                if isinstance(m.n, int) and m.n == STEPS - 1:
                    return
                pool.wait_ge(rstd_done, m.n + 1)
                pool.sem_inc(passed, 1)
                for t in range(HALF):
                    nc.gpsimd.tensor_scalar(y[:, m.u, t, :], y[:, m.u, t, :], mv[:, t, 0:1], rstd[:, t:t + 1],
                                            ALU.subtract, ALU.mult).then_inc(ln_done, 1)

            def step(s):
                if s.live(STEPS):
                    unit_vectors(s)
                if s.after(-1).live(STEPS):
                    bias_residual(s.after(-1))
                if s.after(-2).live(STEPS):
                    layernorm(s.after(-2))

            run(pool, step)

        @block.scalar
        def _(act):
            def copy_xT(m):
                act.wait_ge(xT_ps, m.n + 1)
                nc.scalar.activation(xT[:, m.u, :], turned[:, :], ACT.Copy).then_inc(xT_sb, 1)

            def copy_w(m):
                act.wait_ge(w_done, m.n + 1)
                for b in range(2):
                    nc.scalar.activation(own_w[:, b, :, :].rearrange("p t d -> p (t d)"), w_ps[b][:, :], ACT.Copy)\
                      .then_inc(w_sb, 1)

            def squares(m):
                act.wait_ge(qkv_sb, 3 * HALF * (m.n + 1))
                if m.from_(1):
                    act.wait_ge(summed, m.n)
                nc.scalar.activation(sq[:, :], qk[:, m.u, :, :].rearrange("p t d -> p (t d)"), ACT.Square)\
                  .then_inc(squared, 1)

            def roots(m):
                act.wait_ge(summed, m.n + 1)
                if m.from_(1):
                    act.wait_ge(clamped, m.n)
                nc.scalar.activation(length[:, :], ss[:, :], ACT.Sqrt).then_inc(rooted, 1)

            def copy_qT(m):
                act.wait_ge(qT_ps, m.n + 1)
                nc.scalar.activation(qT[:, m.u, :], turned[:, :], ACT.Copy).then_inc(qT_sb, 1)

            def step(s):
                if s.after(2).live(STEPS):
                    copy_xT(s.after(2))
                if s.after(1).live(STEPS):
                    squares(s.after(1))
                if s.after(-1).live(STEPS):
                    copy_w(s.after(-1))
                if s.after(1).live(STEPS):
                    roots(s.after(1))
                if s.live(STEPS):
                    copy_qT(s)

            run(act, step)

        @block.vector
        def _(dve):
            def add_biases(m):
                for t in range(HALF):
                    dve.wait_ge(qkv_done, HALF * m.n + t + 1)
                    src = qkv_ps[t % 2]
                    nc.vector.tensor_tensor(qk[:, m.u, t, :], src[:, 0:256], bias[:, 0:2, :].rearrange("p n d -> p (n d)"),
                                            ALU.add).then_inc(qkv_sb, 1)
                    for b in range(2):
                        own = slice(64 * b, 64 * b + 64)
                        nc.vector.tensor_tensor(v_z[own, m.u, b, t, :], src[own, 256:384], bias[own, 2, :],
                                                ALU.add).then_inc(qkv_sb, 1)

            def sum_squares(m):
                dve.wait_ge(squared, m.n + 1)
                if m.from_(1):
                    dve.wait_ge(rooted, m.n)
                nc.vector.tensor_reduce(ss[:, :], sq[:, :].rearrange("p (a d) -> p a d", d=HD), AX.X, ALU.add)\
                  .then_inc(summed, 1)

            def invert_lengths(m):
                dve.wait_ge(rooted, m.n + 1)
                if m.from_(1):
                    dve.wait_ge(inv_done, m.n)
                nc.vector.tensor_scalar(inv[:, m.u, :], length[:, :], NORM_EPS, None, ALU.max).then_inc(clamped, 1)
                dve.wait_ge(clamped, m.n + 1)
                nc.vector.reciprocal(inv[:, m.u, :], inv[:, m.u, :]).then_inc(inv_done, 1)

            def keep_heads(m):
                dve.wait_ge(vk_done, m.n + 1)
                for b in range(2):
                    nc.vector.tensor_tensor(vk[:, m.u, b, :, :], vk_ps[b][:, :].rearrange("p (t d) -> p t d", d=P),
                                            own_head[:, :, :].rearrange("p h d -> p (h d)").unsqueeze(1)
                                            .to_broadcast([P, HALF, P]), ALU.mult).then_inc(vk_sb, 1)

            def residual(m):
                dve.wait_ge(y_done, m.n + 1)
                dve.wait_ge(res_biased, m.n + 1)
                dve.sem_inc(passed, 1)
                if m.from_(2):
                    dve.wait_ge(stored[m.u], DMA * m.i)
                nc.vector.tensor_tensor(y[:, m.u, :, :], y_ps[:, :].rearrange("p (t d) -> p t d", d=P),
                                        x_res[:, m.u, :, :], ALU.add).then_inc(res_done, 1)

            def moments(m):
                dve.wait_ge(res_done, m.n + 1)
                for t in range(HALF):
                    nc.vector.bn_stats(stats[:, t, :], y[:, m.u, t, :]).then_inc(stat_done, 1)
                dve.wait_ge(stat_done, HALF * (m.n + 1))
                dve.sem_inc(passed, 1)
                if m.from_(1):
                    dve.wait_ge(ln_done, HALF * m.n)
                    dve.sem_inc(passed, 1)
                for t in range(HALF):
                    ins = nc.vector.bn_aggr(mv[:, t, :], stats[:, t, :])
                ins.then_inc(mv_done, 1)

            def step(s):
                if s.after(-1).live(STEPS):
                    keep_heads(s.after(-1))
                if s.after(1).live(STEPS):
                    add_biases(s.after(1))
                if s.after(-2).live(STEPS):
                    residual(s.after(-2))
                if s.after(1).live(STEPS):
                    sum_squares(s.after(1))
                if s.after(-2).live(STEPS):
                    moments(s.after(-2))
                if s.after(1).live(STEPS):
                    invert_lengths(s.after(1))

            run(dve, step)

            m = Turn(0, STEPS - 1)
            dve.wait_ge(rstd_done, STEPS)
            for t in range(HALF):
                nc.vector.tensor_scalar(y[:, m.u, t, :], y[:, m.u, t, :], mv[:, t, 0:1], rstd[:, t:t + 1],
                                        ALU.subtract, ALU.mult).then_inc(ln_done, 1)

        @block.tensor
        def _(pe):
            def transpose_x(m):
                pe.wait_ge(x_loaded[m.u], DMA * (m.i + 1))
                if m.from_(3):
                    pe.wait_ge(qT_sb, m.n - 2)
                elif m.n:
                    pe.wait_ge(xT_sb, m.n)
                for t in range(HALF):
                    ins = nc.tensor.transpose(turned[:, P * t:P * t + P], x_sb[:, m.u, t, :], c.ident[:, :])
                ins.then_inc(xT_ps, 1)

            def project(m):
                pe.wait_ge(xT_sb, m.n + 1)
                for t in range(HALF):
                    if t >= 2 or m.from_(1):
                        pe.wait_ge(qkv_sb, 3 * (HALF * m.n + t - 1))
                    nc.tensor.matmul(qkv_ps[t % 2][:, 0:384], xT[:, m.u, P * t:P * t + P],
                                     wqkv[:, :, :].rearrange("p n d -> p (n d)"), start=True, stop=True)\
                      .then_inc(qkv_done, 1)

            def transpose_q(m):
                pe.wait_ge(unit_done, m.n + 1)
                if m.after(2).live(STEPS):
                    pe.wait_ge(xT_sb, m.n + 3)
                else:
                    pe.wait_ge(qT_sb, m.n)
                for t in range(HALF):
                    ins = nc.tensor.transpose(turned[:, P * t:P * t + P], qk[:, m.u, t, 0:P], c.ident[:, :])
                ins.then_inc(qT_ps, 1)

            def values_by_keys(m):
                if m.from_(1):
                    pe.wait_ge(vk_sb, 2 * m.n)
                for b in range(2):
                    for t in range(HALF):
                        ins = nc.tensor.matmul(vk_ps[b][:, P * t:P * t + P], v_z[:, m.u, b, t, :], qk[:, m.u, t, P:2 * P],
                                               start=True, stop=True)
                ins.then_inc(vk_done, 1)

            def own_weights(m):
                pe.wait_ge(vk_sb, 2 * m.n + 2)
                if m.from_(1):
                    pe.wait_ge(w_sb, 2 * m.n)
                for b in range(2):
                    for t in range(HALF):
                        ins = nc.tensor.matmul(w_ps[b][:, P * t:P * t + P], vk[:, m.u, b, t, :], wo[:, :],
                                               start=True, stop=True)
                ins.then_inc(w_done, 1)

            def outputs(m):
                pe.wait_ge(w_sb, 2 * m.n + 2)
                pe.wait_ge(qT_sb, m.n + 1)
                if m.from_(1):
                    pe.wait_ge(res_done, m.n)
                for t in range(HALF):
                    for b in range(2):
                        ins = nc.tensor.matmul(y_ps[64 * b:64 * b + 64, P * t:P * t + P],
                                               qT[:, m.u, P * t + S * b:P * t + S * b + S], own_w[:, b, t, :],
                                               start=True, stop=True)
                ins.then_inc(y_done, 1)

            def step(s):
                if s.after(2).live(STEPS):
                    transpose_x(s.after(2))
                if s.after(1).live(STEPS):
                    project(s.after(1))
                if s.after(-1).live(STEPS):
                    own_weights(s.after(-1))
                if s.live(STEPS):
                    transpose_q(s)
                    values_by_keys(s)
                if s.after(-1).live(STEPS):
                    outputs(s.after(-1))

            run(pe, step)


EXPERTS, FF, CAPACITY = 8, 512, 80
CHUNKS = FF // P
GELU_CUBE = 0.044715
GELU_SLOPE = 2.0 * math.sqrt(2.0 / math.pi)
ONE, TILE, ROW, GATE, SENT = 0, 1, 2, 3, 6


def moe_layer(nc, c, tag, x_in, x_out, w):
    STEPS = TILES // HALF
    AHEAD = 4
    with ExitStack() as ctx:
        def sb(name, shape, dt=F32):
            return ctx.enter_context(nc.sbuf_tensor(f"{tag}_{name}", shape, dt))

        def ps(name, shape):
            return ctx.enter_context(nc.psum_tensor(f"{tag}_{name}", shape, F32))

        sem = ctx.enter_context(Semaphores(nc, tag))

        def sem2(name):
            return [sem(f"{name}{u}") for u in range(2)]

        gate_w = sb("gate_w", [P, EXPERTS])
        gate_row = sb("gate_row", [1, EXPERTS])
        gate_b = sb("gate_b", [P, EXPERTS])
        b1_rows = sb("b1_rows", [EXPERTS * CHUNKS, P])
        b1_cols = sb("b1_cols", [P, EXPERTS * CHUNKS])
        upto = sb("upto", [P, P], BF16)
        before = sb("before", [TILES, TILES], BF16)
        ones_b = sb("ones_b", [P, P], BF16)
        rank = sb("rank", [P, EXPERTS])
        slot_row = sb("slot_row", [P, P])
        neg_half = sb("neg_half", [P, 8])

        x_sb = sb("x", [P, AHEAD, HALF, P])
        xT = sb("xT", [P, 2, HALF * P])
        y = sb("y", [P, 2, HALF, P])
        stats = sb("stats", [P, 8, 6])
        mv = sb("mv", [P, 8, 2])
        var_eps, rstd = sb("var_eps", [P, 8]), sb("rstd", [P, 8])
        logits = sb("logits", [P, TILES, EXPERTS])
        expo = sb("expo", [P, TILES, EXPERTS])
        ranked = sb("ranked", [P, TILES, EXPERTS])
        one_hot = sb("one_hot", [P, TILES, EXPERTS], BF16)
        per_tile = sb("per_tile", [TILES, TILES, EXPERTS], BF16)
        top = sb("top", [P, TILES])
        best = sb("best", [P, TILES])
        gate, rest = sb("gate", [P, TILES]), sb("rest", [P, TILES])
        place = sb("place", [P, TILES])
        info = sb("info", [P, TILES, SENT], BF16)
        send = sb("send", [P, TILES, EXPERTS, SENT], BF16)
        at_slot = sb("at_slot", [P, TILES, P], BF16)
        slot_info = sb("slot_info", [P, EXPERTS, SENT])
        token_f, out_f = sb("token_f", [P, EXPERTS]), sb("out_f", [P, EXPERTS])
        token, out_row = sb("token", [P, EXPERTS], U32), sb("out_row", [P, EXPERTS], U32)
        slot_gate = sb("slot_gate", [P, EXPERTS])

        w1 = sb("w1", [P, EXPERTS, FF])
        w2 = sb("w2", [P, EXPERTS, CHUNKS, P])
        b2 = sb("b2", [1, EXPERTS, P])
        xd = sb("xd", [P, EXPERTS, P])
        xdT = sb("xdT", [P, 2, P])
        hid, hid_sq, hid_w, sig = (sb(n, [P, 2, FF]) for n in ("hid", "hid_sq", "hid_w", "sig"))
        yd = sb("yd", [P, EXPERTS, P])

        xT_ps = [ps(f"xT_ps{u}", [P, 512]) for u in range(2)]
        l_ps = [ps(f"l_ps{u}", [P, 512]) for u in range(2)]
        h_ps = [ps(f"h_ps{u}", [P, 512]) for u in range(2)]
        o_ps = [ps(f"o_ps{u}", [P, 512]) for u in range(2)]

        w_loaded, filled, picked, cols, biased = map(sem, ("w_loaded", "filled", "picked", "cols", "biased"))
        x_loaded = [sem(f"x_loaded{v}") for v in range(AHEAD)]
        stored, gathered = map(sem2, ("stored", "gathered"))
        e_loaded = sem("e_loaded")
        turned, turned_sb, gated, logit_done = map(sem, ("turned", "turned_sb", "gated", "logit_done"))
        stat_done, mv_done, eps_done, rstd_done, ln_done = map(
            sem, ("stat_done", "mv_done", "eps_done", "rstd_done", "ln_done"))
        routed, expo_done, counted, ranked_ps, slot_ready, sent = map(
            sem, ("routed", "expo_done", "counted", "ranked_ps", "slot_ready", "sent"))
        passed = sem("passed")

        def run(eng, step):
            rounds = (STEPS - (AHEAD - 1)) // AHEAD
            for k in range(-2, AHEAD):
                step(Turn(0, k, AHEAD))
            with eng.Fori(1, rounds) as i:
                for v in range(AHEAD):
                    step(Turn(i, v, AHEAD))
            for k in range(AHEAD * rounds, STEPS + 1):
                step(Turn(0, k, AHEAD))

        with nc.Block() as block:
            @block.sync
            def _(sp):
                sp.dma_start(gate_w[:, :], w["gate_w"]).then_inc(w_loaded, DMA)
                sp.dma_start(gate_row[:, :], w["gate_b"].rearrange("(a e) -> a e", a=1)).then_inc(w_loaded, DMA)
                sp.dma_start(b1_rows[:, :], w["b1"].rearrange("e (c f) -> (e c) f", f=P)).then_inc(w_loaded, DMA)
                for m in range(AHEAD):
                    sp.dma_start(x_sb[:, m, :, :], quarter_tiles(x_in, m)).then_inc(x_loaded[m], DMA)
                sp.wait_ge(w_loaded, 3 * DMA)

            @block.vector
            def _(dve):
                nc.vector.memset(upto[:, :], 1.0).then_inc(filled, 1)
                nc.vector.memset(before[:, :], 1.0).then_inc(filled, 1)
                nc.vector.memset(ones_b[:, :], 1.0).then_inc(filled, 1)
                nc.vector.memset(neg_half[:, :], -0.5).then_inc(filled, 1)
                nc.vector.memset(slot_row[:, CAPACITY:P], -1.0).then_inc(filled, 1)
                for e in range(EXPERTS):
                    nc.vector.memset(rank[:, e:e + 1], float(EXPERTS - e)).then_inc(filled, 1)
                nc.vector.memset(info[:, :, ONE], 1.0).then_inc(filled, 1)
                dve.wait_ge(cols, 1)
                nc.vector.tensor_copy(gate_b[:, :], l_ps[0][:, 0:EXPERTS]).then_inc(biased, 1)
                nc.vector.tensor_copy(b1_cols[:, :], l_ps[1][:, 0:EXPERTS * CHUNKS]).then_inc(biased, 1)
                dve.wait_ge(cols, 2)
                nc.vector.tensor_copy(info[:, :, ROW], h_ps[0][:, 0:TILES]).then_inc(biased, 1)
                nc.vector.tensor_copy(info[:, :, TILE], h_ps[1][:, 0:TILES]).then_inc(biased, 1)
                nc.vector.tensor_copy(slot_row[:, 0:CAPACITY], o_ps[0][:, 0:CAPACITY]).then_inc(biased, 1)

            @block.gpsimd
            def _(pool):
                pool.wait_ge(filled, 3)
                nc.gpsimd.affine_select(out=upto[:, :], in_=upto[:, :], compare_op=ALU.is_ge, fill=0.0,
                                        base=0, pattern=[[1, P]], channel_multiplier=-1).then_inc(picked, 1)
                pool.wait_ge(picked, 1)
                nc.gpsimd.affine_select(out=before[:, :], in_=before[:, :], compare_op=ALU.is_ge, fill=0.0,
                                        base=-1, pattern=[[1, TILES]], channel_multiplier=-1).then_inc(picked, 1)
                pool.wait_ge(picked, 2)

            @block.tensor
            def _(pe):
                pe.wait_ge(w_loaded, 3 * DMA)
                nc.tensor.matmul(l_ps[0][:, 0:EXPERTS], c.ones_row[0:1, :], gate_row[:, :], start=True, stop=True)
                nc.tensor.transpose(l_ps[1][:, 0:EXPERTS * CHUNKS], b1_rows[:, :],
                                    c.ident[0:EXPERTS * CHUNKS, 0:EXPERTS * CHUNKS]).then_inc(cols, 1)
                pe.wait_ge(picked, 2)
                nc.tensor.matmul(h_ps[0][:, 0:TILES], upto[:, :], ones_b[:, 0:TILES], start=True, stop=True)
                nc.tensor.matmul(h_ps[1][:, 0:TILES], ones_b[0:TILES, :], before[:, :], start=True, stop=True)
                nc.tensor.matmul(o_ps[0][:, 0:P], ones_b[:, :], upto[:, :], start=True, stop=True).then_inc(cols, 1)

        with nc.Block() as block:
            @block.sync
            def _(sp):
                def load_x(m):
                    if m.from_(AHEAD):
                        sp.wait_ge(turned, m.n - AHEAD + 1)
                        sp.sem_inc(passed, 1)
                        sp.wait_ge(ln_done, HALF * (m.n - AHEAD + 1))
                        sp.sem_inc(passed, 1)
                        sp.dma_start(x_sb[:, m.v, :, :], quarter_tiles(x_in, m.n)).then_inc(x_loaded[m.v], DMA)

                def store(m):
                    sp.wait_ge(ln_done, HALF * (m.n + 1))
                    sp.sem_inc(passed, 1)
                    sp.dma_start(quarter_tiles(x_out, m.n), y[:, m.u, :, :]).then_inc(stored[m.u], DMA)

                def step(s):
                    if s.after(AHEAD - 1).live(STEPS):
                        load_x(s.after(AHEAD - 1))
                    if s.after(-1).live(STEPS):
                        store(s.after(-1))

                run(sp, step)
                for u in range(2):
                    sp.wait_ge(stored[u], DMA * STEPS // 2)

            @block.scalar
            def _(act):
                def copy_xT(m):
                    act.wait_ge(turned, m.n + 1)
                    if m.from_(2):
                        act.wait_ge(gated, m.n - 1)
                    nc.scalar.activation(xT[:, m.u, :], xT_ps[m.u][:, :], ACT.Copy).then_inc(turned_sb, 1)

                run(act, lambda s: copy_xT(s) if s.live(STEPS) else None)

            @block.tensor
            def _(pe):
                def turn(m):
                    pe.wait_ge(x_loaded[m.v], DMA * (m.j + 1))
                    if m.from_(2):
                        pe.wait_ge(turned_sb, m.n - 1)
                    for t in range(HALF):
                        ins = nc.tensor.transpose(xT_ps[m.u][:, P * t:P * t + P], x_sb[:, m.v, t, :], c.ident[:, :])
                    ins.then_inc(turned, 1)

                def gates(m):
                    pe.wait_ge(turned_sb, m.n + 1)
                    if m.from_(2):
                        pe.wait_ge(logit_done, m.n - 1)
                    for t in range(HALF):
                        ins = nc.tensor.matmul(l_ps[m.u][:, EXPERTS * t:EXPERTS * t + EXPERTS],
                                               xT[:, m.u, P * t:P * t + P], gate_w[:, :], start=True, stop=True)
                    ins.then_inc(gated, 1)

                def step(s):
                    if s.after(1).live(STEPS):
                        turn(s.after(1))
                    if s.live(STEPS):
                        gates(s)

                run(pe, step)

            @block.vector
            def _(dve):
                def moments(m):
                    dve.wait_ge(x_loaded[m.v], DMA * (m.j + 1))
                    if m.from_(1):
                        dve.wait_ge(mv_done, m.n)
                    for t in range(HALF):
                        nc.vector.bn_stats(stats[:, t, :], x_sb[:, m.v, t, :]).then_inc(stat_done, 1)
                    dve.wait_ge(stat_done, HALF * (m.n + 1))
                    dve.sem_inc(passed, 1)
                    if m.from_(2):
                        dve.wait_ge(ln_done, HALF * (m.n - 1))
                        dve.sem_inc(passed, 1)
                    for t in range(HALF):
                        ins = nc.vector.bn_aggr(mv[:, HALF * m.u + t, :], stats[:, t, :])
                    ins.then_inc(mv_done, 1)

                def normalise(m):
                    dve.wait_ge(rstd_done, m.n + 1)
                    dve.sem_inc(passed, 1)
                    if m.from_(2):
                        dve.wait_ge(stored[m.u], DMA * m.i)
                        dve.sem_inc(passed, 1)
                    for t in range(HALF):
                        k = HALF * m.u + t
                        nc.vector.tensor_scalar(y[:, m.u, t, :], x_sb[:, m.v, t, :], mv[:, k, 0:1], rstd[:, k:k + 1],
                                                ALU.subtract, ALU.mult).then_inc(ln_done, 1)

                def add_bias(m):
                    dve.wait_ge(gated, m.n + 1)
                    nc.vector.tensor_tensor(logits[:, bass.ds(HALF * m.n, HALF), :],
                                            l_ps[m.u][:, 0:HALF * EXPERTS].rearrange("p (t e) -> p t e", e=EXPERTS),
                                            gate_b[:, :].unsqueeze(1).to_broadcast([P, HALF, EXPERTS]), ALU.add)\
                      .then_inc(logit_done, 1)

                def step(s):
                    if s.live(STEPS):
                        normalise(s)
                    if s.after(2).live(STEPS):
                        moments(s.after(2))
                    if s.live(STEPS):
                        add_bias(s)

                run(dve, step)

            @block.gpsimd
            def _(pool):
                def deviations(m):
                    r = slice(HALF * m.u, HALF * m.u + HALF)
                    pool.wait_ge(mv_done, m.n + 1)
                    pool.sem_inc(passed, 1)
                    nc.gpsimd.tensor_scalar(var_eps[:, r], mv[:, r, 1], LN_EPS, None, ALU.add).then_inc(eps_done, 1)
                    pool.wait_ge(eps_done, m.n + 1)
                    nc.gpsimd.tensor_tensor(rstd[:, r], var_eps[:, r], neg_half[:, r], ALU.pow).then_inc(rstd_done, 1)

                run(pool, lambda s: deviations(s) if s.live(STEPS) else None)

        with nc.Block() as block:
            QUARTER = TILES // 4

            def over_experts(a):
                return a[:, :].unsqueeze(2).to_broadcast([P, TILES, EXPERTS])

            def over_tiles(a):
                return a[:, :].unsqueeze(1).to_broadcast([P, TILES, EXPERTS])

            @block.sync
            def _(sp):
                sp.dma_start(w1[:, :, :], w["w1"].rearrange("e d f -> d e f")).then_inc(e_loaded, DMA)
                sp.dma_start(w2[:, :, :, :], w["w2"].rearrange("e (c f) d -> f e c d", f=P)).then_inc(e_loaded, DMA)
                sp.dma_start(b2[0:1, :, :], w["b2"].rearrange("(a e) d -> a e d", a=1)).then_inc(e_loaded, DMA)

            @block.vector
            def _(dve):
                nc.vector.tensor_reduce(top[:, :], logits[:, :, :], AX.X, ALU.max).then_inc(routed, 1)
                dve.wait_ge(routed, 1)
                nc.vector.tensor_tensor(logits[:, :, :], logits[:, :, :], over_experts(top), ALU.subtract)\
                  .then_inc(routed, 1)
                dve.wait_ge(routed, 2)
                nc.vector.scalar_tensor_tensor(out=ranked[:, :, :], in0=logits[:, :, :], scalar=0.0,
                                               in1=over_tiles(rank), op0=ALU.is_ge, op1=ALU.mult).then_inc(routed, 1)
                dve.wait_ge(routed, 3)
                nc.vector.tensor_reduce(best[:, :], ranked[:, :, :], AX.X, ALU.max).then_inc(routed, 1)
                dve.wait_ge(routed, 4)
                nc.vector.tensor_tensor(one_hot[:, :, :], over_tiles(rank), over_experts(best), ALU.is_equal)\
                  .then_inc(routed, 1)
                dve.wait_ge(expo_done, 1)
                nc.vector.tensor_reduce(gate[:, :], expo[:, :, :], AX.X, ALU.add).then_inc(routed, 1)
                dve.wait_ge(routed, 6)
                nc.vector.reciprocal(gate[:, :], gate[:, :]).then_inc(routed, 1)
                dve.wait_ge(counted, 1)
                nc.vector.tensor_tensor(per_tile[:, :, :],
                                        before[:, :].unsqueeze(2).to_broadcast([TILES, TILES, EXPERTS]),
                                        l_ps[0][0:TILES, 0:EXPERTS].unsqueeze(1).to_broadcast([TILES, TILES, EXPERTS]),
                                        ALU.mult).then_inc(ranked_ps, 1)
                dve.wait_ge(routed, 7)
                nc.vector.tensor_copy(info[:, :, GATE], gate[:, :]).then_inc(routed, 1)
                dve.wait_ge(routed, 8)
                nc.vector.tensor_tensor(rest[:, :], gate[:, :], info[:, :, GATE], ALU.subtract).then_inc(routed, 1)
                dve.wait_ge(routed, 9)
                nc.vector.tensor_copy(info[:, :, GATE + 1], rest[:, :]).then_inc(routed, 1)
                dve.wait_ge(routed, 10)
                nc.vector.tensor_tensor(info[:, :, GATE + 2], rest[:, :], info[:, :, GATE + 1], ALU.subtract)\
                  .then_inc(routed, 1)
                dve.wait_ge(routed, 11)
                wide = [P, TILES, EXPERTS, SENT]
                nc.vector.tensor_tensor(send[:, :, :, :], info[:, :, :].unsqueeze(2).to_broadcast(wide),
                                        one_hot[:, :, :].unsqueeze(3).to_broadcast(wide), ALU.mult).then_inc(routed, 1)
                dve.wait_ge(counted, 2)
                nc.vector.tensor_tensor(ranked[:, :, :], one_hot[:, :, :],
                                        l_ps[1][:, :].rearrange("p (t e) -> p t e", e=EXPERTS), ALU.mult).then_inc(routed, 1)
                dve.wait_ge(routed, 13)
                nc.vector.tensor_reduce(place[:, :], ranked[:, :, :], AX.X, ALU.add).then_inc(routed, 1)
                dve.wait_ge(routed, 14)
                for q in range(4):
                    part = slice(QUARTER * q, QUARTER * q + QUARTER)
                    shape = [P, QUARTER, P]
                    nc.vector.tensor_tensor(at_slot[:, part, :], slot_row[:, :].unsqueeze(1).to_broadcast(shape),
                                            place[:, part].unsqueeze(2).to_broadcast(shape), ALU.is_equal)\
                      .then_inc(slot_ready, 1)
                dve.wait_ge(sent, 1)
                nc.vector.tensor_copy(slot_info[:, :, :], o_ps[0][:, 0:EXPERTS * SENT].rearrange("p (e s) -> p e s", s=SENT))\
                  .then_inc(routed, 1)
                dve.wait_ge(routed, 15)
                nc.vector.scalar_tensor_tensor(out=token_f[:, :], in0=slot_info[:, :, TILE], scalar=float(P),
                                               in1=slot_info[:, :, ROW], op0=ALU.mult, op1=ALU.add).then_inc(routed, 1)
                nc.vector.tensor_tensor(slot_gate[:, :], slot_info[:, :, GATE + 1], slot_info[:, :, GATE + 2], ALU.add)\
                  .then_inc(routed, 1)
                dve.wait_ge(routed, 17)
                nc.vector.tensor_tensor(slot_gate[:, :], slot_gate[:, :], slot_info[:, :, GATE], ALU.add).then_inc(routed, 1)
                nc.vector.tensor_tensor(token_f[:, :], token_f[:, :], slot_info[:, :, ONE], ALU.subtract).then_inc(routed, 1)
                nc.vector.tensor_scalar(out_f[:, :], slot_info[:, :, ONE], -float(B * S), float(B * S),
                                        ALU.mult, ALU.add).then_inc(routed, 1)
                dve.wait_ge(routed, 20)
                nc.vector.tensor_tensor(out_f[:, :], out_f[:, :], token_f[:, :], ALU.add).then_inc(routed, 1)
                nc.vector.tensor_copy(token[:, :], token_f[:, :]).then_inc(routed, 1)
                dve.wait_ge(routed, 22)
                nc.vector.tensor_copy(out_row[:, :], out_f[:, :]).then_inc(routed, 1)
                dve.wait_ge(routed, 23)

            @block.scalar
            def _(act):
                act.wait_ge(routed, 2)
                nc.scalar.activation(expo[:, :, :], logits[:, :, :], ACT.Exp).then_inc(expo_done, 1)

            @block.tensor
            def _(pe):
                pe.wait_ge(routed, 5)
                for e in range(EXPERTS):
                    ins = nc.tensor.matmul(l_ps[0][0:TILES, e:e + 1], one_hot[:, :, e], ones_b[:, 0:1],
                                           start=True, stop=True)
                ins.then_inc(counted, 1)
                nc.tensor.matmul(l_ps[1][:, :], upto[:, :], one_hot[:, :, :].rearrange("p t e -> p (t e)"),
                                 start=True, stop=False)
                pe.wait_ge(ranked_ps, 1)
                nc.tensor.matmul(l_ps[1][:, :], ones_b[0:TILES, :], per_tile[:, :, :].rearrange("p t e -> p (t e)"),
                                 start=False, stop=True).then_inc(counted, 1)
                for t in range(TILES):
                    if t % QUARTER == 0:
                        pe.wait_ge(slot_ready, t // QUARTER + 1)
                    ins = nc.tensor.matmul(o_ps[0][:, 0:EXPERTS * SENT], at_slot[:, t, :],
                                           send[:, t, :, :].rearrange("p e s -> p (e s)"),
                                           start=(t == 0), stop=(t == TILES - 1))
                ins.then_inc(sent, 1)

        (e_turned, e_turned_sb, h_done, h_biased, h_squared, h_inner, h_sig, h_ready, o_done, h_cubed, added) = map(
            sem, ("e_turned", "e_turned_sb", "h_done", "h_biased", "h_squared", "h_inner", "h_sig", "h_ready",
                  "o_done", "h_cubed", "added"))
        d_stat, d_mv, d_eps, d_rstd, d_normed, scattered = map(
            sem, ("d_stat", "d_mv", "d_eps", "d_rstd", "d_normed", "scattered"))

        def experts(step):
            for k in range(-1, EXPERTS + 1):
                step(Turn(0, k))

        block = ctx.enter_context(nc.Block())

        @block.gpsimd
        def _(pool):
            for e in range(EXPERTS):
                if e >= 2:
                    pool.wait_ge(gathered[e % 2], DMA * (e // 2))
                nc.gpsimd.indirect_dma_start(
                    out=xd[:, e, :], out_offset=None, in_=x_in[:, :],
                    in_offset=bass.IndirectOffsetOnAxis(ap=token[:, e:e + 1], axis=0),
                    bounds_check=B * S - 1, oob_is_err=False).then_inc(gathered[e % 2], DMA)
            pool.wait_ge(d_mv, 1)
            nc.gpsimd.tensor_scalar(var_eps[:, :], mv[:, :, 1], LN_EPS, None, ALU.add).then_inc(d_eps, 1)
            pool.wait_ge(d_eps, 1)
            nc.gpsimd.tensor_tensor(rstd[:, :], var_eps[:, :], neg_half[:, :], ALU.pow).then_inc(d_rstd, 1)
            for e in range(EXPERTS):
                pool.wait_ge(d_normed, e + 1)
                nc.gpsimd.indirect_dma_start(
                    out=x_out[:, :], out_offset=bass.IndirectOffsetOnAxis(ap=out_row[:, e:e + 1], axis=0),
                    in_=yd[:, e, :], in_offset=None, bounds_check=B * S - 1, oob_is_err=False).then_inc(scattered, DMA)
            pool.wait_ge(scattered, DMA * EXPERTS)

        @block.scalar
        def _(act):
            def take_in(m):
                u = m.u
                act.wait_ge(e_turned, m.n + 1)
                if m.from_(2):
                    act.wait_ge(h_done, m.n - 1)
                nc.scalar.activation(xdT[:, u, :], xT_ps[u][:, 0:P], ACT.Copy).then_inc(e_turned_sb, 1)
                act.wait_ge(h_biased, m.n + 1)
                nc.scalar.activation(hid_sq[:, u, :], hid[:, u, :], ACT.Square).then_inc(h_squared, 1)

            def sigmoid(m):
                act.wait_ge(h_inner, m.n + 1)
                nc.scalar.activation(sig[:, m.u, :], hid_w[:, m.u, :], ACT.Sigmoid, scale=GELU_SLOPE).then_inc(h_sig, 1)

            def step(s):
                if s.live(EXPERTS):
                    sigmoid(s)
                if s.after(1).live(EXPERTS):
                    take_in(s.after(1))

            experts(step)

        @block.vector
        def _(dve):
            def bias(m):
                u = m.u
                dve.wait_ge(h_done, m.n + 1)
                if m.from_(2):
                    dve.wait_ge(o_done, m.n - 1)
                nc.vector.tensor_tensor(hid[:, u, :].rearrange("p (c s) -> p c s", s=P),
                                        h_ps[u][:, :].rearrange("p (c s) -> p c s", s=P),
                                        b1_cols[:, CHUNKS * m.n:CHUNKS * m.n + CHUNKS].unsqueeze(2)
                                        .to_broadcast([P, CHUNKS, P]), ALU.add).then_inc(h_biased, 1)

            def inner(m):
                u = m.u
                dve.wait_ge(h_squared, m.n + 1)
                nc.vector.tensor_scalar(hid_sq[:, u, :], hid_sq[:, u, :], GELU_CUBE, 1.0, ALU.mult, ALU.add)\
                  .then_inc(h_cubed, 1)
                dve.wait_ge(h_cubed, m.n + 1)
                nc.vector.tensor_tensor(hid_w[:, u, :], hid_sq[:, u, :], hid[:, u, :], ALU.mult).then_inc(h_inner, 1)

            def gelu(m):
                u = m.u
                dve.wait_ge(h_sig, m.n + 1)
                nc.vector.tensor_tensor(hid[:, u, :], hid[:, u, :], sig[:, u, :], ALU.mult).then_inc(h_ready, 1)

            def add(m):
                dve.wait_ge(o_done, m.n + 1)
                nc.vector.scalar_tensor_tensor(out=yd[:, m.n, :], in0=o_ps[m.u][:, 0:P], scalar=slot_gate[:, m.n:m.n + 1],
                                               in1=xd[:, m.n, :], op0=ALU.mult, op1=ALU.add).then_inc(added, 1)

            def step(s):
                if s.after(1).live(EXPERTS):
                    bias(s.after(1))
                if s.live(EXPERTS):
                    gelu(s)
                if s.after(1).live(EXPERTS):
                    inner(s.after(1))
                if s.after(-1).live(EXPERTS):
                    add(s.after(-1))

            experts(step)
            dve.wait_ge(added, EXPERTS)
            for e in range(EXPERTS):
                nc.vector.bn_stats(stats[:, e, :], yd[:, e, :]).then_inc(d_stat, 1)
            dve.wait_ge(d_stat, EXPERTS)
            for e in range(EXPERTS):
                ins = nc.vector.bn_aggr(mv[:, e, :], stats[:, e, :])
            ins.then_inc(d_mv, 1)
            dve.wait_ge(d_rstd, 1)
            dve.wait_ge(d_mv, 1)
            for e in range(EXPERTS):
                nc.vector.tensor_scalar(yd[:, e, :], yd[:, e, :], mv[:, e, 0:1], rstd[:, e:e + 1],
                                        ALU.subtract, ALU.mult).then_inc(d_normed, 1)

        @block.tensor
        def _(pe):
            def up(m):
                u = m.u
                pe.wait_ge(gathered[u], DMA * (m.i + 1))
                nc.tensor.transpose(xT_ps[u][:, 0:P], xd[:, m.n, :], c.ident[:, :]).then_inc(e_turned, 1)
                pe.wait_ge(e_turned_sb, m.n + 1)
                pe.wait_ge(e_loaded, 3 * DMA)
                if m.from_(2):
                    pe.wait_ge(h_biased, m.n - 1)
                for k in range(CHUNKS):
                    ins = nc.tensor.matmul(h_ps[u][:, P * k:P * k + P], w1[:, m.n, P * k:P * k + P], xdT[:, u, :],
                                           start=True, stop=True)
                ins.then_inc(h_done, 1)

            def down(m):
                u = m.u
                pe.wait_ge(h_ready, m.n + 1)
                if m.from_(2):
                    pe.wait_ge(added, m.n - 1)
                for k in range(CHUNKS):
                    nc.tensor.matmul(o_ps[u][:, 0:P], hid[:, u, P * k:P * k + P], w2[:, m.n, k, :],
                                     start=(k == 0), stop=False)
                nc.tensor.matmul(o_ps[u][:, 0:P], c.ones_row[0:1, :], b2[:, m.n, :], start=False, stop=True)\
                  .then_inc(o_done, 1)

            def step(s):
                if s.after(1).live(EXPERTS):
                    up(s.after(1))
                if s.live(EXPERTS):
                    down(s)

            experts(step)


LATENT = 64
VCOLS = LATENT + 1
HEADS_OF = (range(0, 7), range(7, 14), range(14, 16))
WO_CHUNKS = H * LATENT // P


def latent_attention(nc, c, tag, x_in, x_out, w):
    with ExitStack() as ctx:
        def sb(name, shape, dt=F32):
            return ctx.enter_context(nc.sbuf_tensor(f"{tag}_{name}", shape, dt))

        def ps(name, shape):
            return ctx.enter_context(nc.psum_tensor(f"{tag}_{name}", shape, F32))

        sem = ctx.enter_context(Semaphores(nc, tag))

        def sem2(name):
            return [sem(f"{name}{u}") for u in range(2)]

        wq_p, wk_p = sb("wq_p", [P, P]), sb("wk_p", [P, P])
        wv = sb("wv", [P, H * LATENT])
        wo = sb("wo", [P, WO_CHUNKS, P])
        rows_p = sb("rows_p", [1, 2, P])
        bcol = sb("bcol", [P, 2])
        bo_all = sb("bo_all", [P, P])
        x_sb = sb("x", [P, 2, T, P])
        xT = sb("xT", [P, 2, GT])
        q_hi, q_lo, k_hi, k_lo = (sb(n, [P, GT], F16) for n in ("q_hi", "q_lo", "k_hi", "k_lo"))
        q_st, k_st = c.q_st, c.k_st
        v_hi, v_lo = (sb(n, [P, 4, H, VCOLS], F16) for n in ("v_hi", "v_lo"))
        prob = sb("prob", [P, 2, H, S])
        p_hi, p_lo = (sb(n, [P, 2, H, 2, S], F16) for n in ("p_hi", "p_lo"))
        mt = sb("mt", [P, 32])
        mc = sb("mc", [64, 32], BF16)
        lower = sb("lower", [P, 2, 32, 32], BF16)
        recip = sb("recip", [P, H])
        o_sb = sb("o", [P, 2, H, LATENT])
        oT = sb("oT", [P, WO_CHUNKS, P])
        x_res = sb("x_res", [P, 2, T, P])
        y = sb("y", [P, 2, T, P])
        stats = sb("stats", [P, T, 6])
        mv = sb("mv", [P, 2, T, 2])
        var_eps, rstd, neg_half = sb("var_eps", [P, T]), sb("rstd", [P, T]), sb("neg_half", [P, T])

        score = [ps(f"score{t}", [P, 2, 512]) for t in range(2)]
        bank = [ps(f"bank{k}", [P, 512]) for k in range(2)]
        o_turned = ps("o_turned", [P, 512])
        extra = ps("extra", [P, 512])
        last_heads = extra[:, 0:2 * VCOLS].rearrange("p (h d) -> p h d", d=VCOLS)
        mt_ps = extra[0:64, 160:224]
        y_ps = extra[:, 256:256 + P]

        def values_of(t2, g):
            if g == 2:
                return last_heads
            return score[t2][:, g, 0:7 * VCOLS].rearrange("p (h d) -> p h d", d=VCOLS)

        w_loaded, w_cols, b_ready, cleared = map(sem, ("w_loaded", "w_cols", "b_ready", "cleared"))
        x_loaded, q_placed, k_placed, stored = map(sem2, ("x_loaded", "q_placed", "k_placed", "stored"))
        res_loaded = sem2("res_loaded")
        xT_ps, q_ps, k_ps, v_ps, s_done, mt_done, low_done, av_done, ot_ps, y_done = map(sem, (
            "xT_ps", "q_ps", "k_ps", "v_ps", "s_done", "mt_done", "low_done", "av_done", "ot_ps", "y_done"))
        xT_sb, q_hi_ok, k_hi_ok, v_hi_ok, prob_ok, p_hi_ok, ot_sb = map(sem, (
            "xT_sb", "q_hi_ok", "k_hi_ok", "v_hi_ok", "prob_ok", "p_hi_ok", "ot_sb"))
        q_lo_ok, k_lo_ok, v_lo_ok, max_done, mc_done, lower_done, p_lo0_ok, p_lo1_ok = map(sem, (
            "q_lo_ok", "k_lo_ok", "v_lo_ok", "max_done", "mc_done", "lower_done", "p_lo0_ok", "p_lo1_ok"))
        recip_done, scaled, res_done, stat_done, mv_done = map(sem, (
            "recip_done", "scaled", "res_done", "stat_done", "mv_done"))
        res_biased, eps_done, rstd_done, ln_done = map(sem, ("res_biased", "eps_done", "rstd_done", "ln_done"))
        passed = sem("passed")

        QPLACE, KPLACE = 12, 3
        PARTS = ((q_hi, q_lo, q_hi), (k_hi, k_hi, k_lo))

        with ExitStack() as part:
            def tmp(name, shape):
                return part.enter_context(nc.sbuf_tensor(f"{tag}_{name}", shape, F32))

            wq = tmp("wq", [P, P])
            wk, wkT = y[:, 0, :, :], oT[:, :, :]
            bv_w = x_sb[:, 1, :, :]
            wc2 = tmp("wc2", [HD, 2, LATENT])
            wcT = tmp("wcT", [P, 2, HD])
            vec_rows = tmp("vec_rows", [32, P])
            vec_cols = tmp("vec_cols", [P, 32])
            rows = tmp("rows", [1, 2, P])
            with nc.Block() as block:
                @block.sync
                def _(sp):
                    sp.dma_start(wq[:, :], w["Wq"]).then_inc(w_loaded, DMA)
                    sp.dma_start(wk, w["Wk"].rearrange("i (c d) -> i c d", d=P)).then_inc(w_loaded, DMA)
                    sp.dma_start(wv[:, :], w["Wv"]).then_inc(w_loaded, DMA)
                    sp.dma_start(wo[:, :, :], w["Wo"].rearrange("(c p) o -> p c o", p=P)).then_inc(w_loaded, DMA)
                    for k in range(2):
                        sp.dma_start(wc2[:, k, :], w["Wc"]).then_inc(w_loaded, DMA)
                    for n, name in enumerate(("bq", "bo")):
                        sp.dma_start(rows[0:1, n, :], w[name].rearrange("(a d) -> a d", a=1)).then_inc(w_loaded, DMA)
                    sp.wait_ge(cleared, 1)
                    for n, name in enumerate(("bk", "bv")):
                        sp.dma_start(vec_rows[8 * n:8 * n + 8, :], w[name].rearrange("(c p) -> c p", p=P))\
                          .then_inc(w_loaded, DMA)
                    sp.dma_start(x_sb[:, 0, :, :], tiles_of(x_in, 0)).then_inc(x_loaded[0], DMA)
                    sp.wait_ge(w_loaded, 10 * DMA)

                @block.vector
                def _(dve):
                    nc.vector.memset(vec_rows[:, :], 0.0).then_inc(cleared, 1)
                    nc.vector.memset(wcT[:, :, :], 0.0).then_inc(cleared, 1)
                    nc.vector.memset(lower[:, :, :, :], 0.0).then_inc(cleared, 1)
                    nc.vector.memset(p_hi[:, :, :, :, :].bitcast(F32), 0.0).then_inc(cleared, 1)
                    nc.vector.memset(p_lo[:, :, :, :, :].bitcast(F32), 0.0).then_inc(cleared, 1)
                    nc.vector.memset(v_hi[:, :, :, LATENT:VCOLS], 1.0).then_inc(cleared, 1)
                    nc.vector.memset(v_lo[:, :, :, LATENT:VCOLS], 0.0).then_inc(cleared, 1)
                    nc.vector.memset(neg_half[:, :], -0.5).then_inc(cleared, 1)
                    perm = "k (f h d) -> k h d f"
                    dve.wait_ge(w_loaded, 10 * DMA)
                    scale = float(LATENT) ** -0.5
                    nc.vector.tensor_scalar(wq_p[:, :].rearrange("k (h d f) -> k h d f", h=4, f=4),
                                            wq[:, :].rearrange(perm, h=4, f=4), scale, None, ALU.mult).then_inc(b_ready, 1)
                    nc.vector.tensor_scalar(rows_p[0:1, 0, :].rearrange("k (h d f) -> k h d f", h=4, f=4),
                                            rows[0:1, 0, :].rearrange(perm, h=4, f=4), scale, None, ALU.mult)\
                      .then_inc(b_ready, 1)
                    dve.wait_ge(w_cols, 1)
                    dve.wait_ge(cleared, 2)
                    for k in range(2):
                        half = slice(64 * k, 64 * k + 64)
                        nc.vector.tensor_copy(wcT[half, k, :], extra[half, 0:HD]).then_inc(b_ready, 1)
                    nc.vector.tensor_copy(vec_cols[:, :], o_turned[:, 0:32]).then_inc(b_ready, 1)
                    for k in range(2):
                        nc.vector.tensor_copy(wkT[:, 4 * k:4 * k + 4, :].rearrange("p c i -> p (c i)"), bank[k][:, :])\
                          .then_inc(b_ready, 1)
                    dve.wait_ge(b_ready, 5)
                    nc.vector.tensor_copy(bv_w, vec_cols[:, 8:16].unsqueeze(2).to_broadcast([P, WO_CHUNKS, P]))\
                      .then_inc(b_ready, 1)
                    dve.wait_ge(w_cols, 2)
                    nc.vector.tensor_copy(wk_p[:, :].rearrange("k (h d f) -> k h d f", h=4, f=4),
                                          score[0][:, 0, 0:P].rearrange(perm, h=4, f=4)).then_inc(b_ready, 1)
                    nc.vector.tensor_copy(rows_p[0:1, 1, :].rearrange("k (h d f) -> k h d f", h=4, f=4),
                                          score[0][0:1, 1, 0:P].rearrange(perm, h=4, f=4)).then_inc(b_ready, 1)
                    nc.vector.tensor_copy(bo_all[:, :], score[1][:, 0, 0:P]).then_inc(b_ready, 1)
                    dve.wait_ge(w_cols, 3)
                    nc.vector.tensor_copy(bcol[:, :], score[1][:, 1, 0:2]).then_inc(b_ready, 1)

                @block.tensor
                def _(pe):
                    pe.wait_ge(w_loaded, 10 * DMA)
                    for n in range(WO_CHUNKS):
                        nc.tensor.transpose(bank[n // 4][:, P * (n % 4):P * (n % 4) + P], wk[:, n, :], c.ident[:, :])
                    nc.tensor.transpose(extra[:, 0:HD], wc2[:, :, :].rearrange("d a l -> d (a l)"), c.ident[0:HD, 0:HD])
                    nc.tensor.transpose(o_turned[:, 0:32], vec_rows[:, :], c.ident[0:32, 0:32]).then_inc(w_cols, 1)
                    pe.wait_ge(b_ready, 8)
                    for n in range(WO_CHUNKS):
                        cols = slice(2 * HD * n, 2 * HD * n + 2 * HD)
                        block_c = wcT[:, :, :].rearrange("p a d -> p (a d)")
                        nc.tensor.matmul(score[0][:, 0, cols], wkT[:, n, :], block_c, start=True, stop=True)
                        nc.tensor.matmul(score[0][0:1, 1, cols], vec_cols[:, n:n + 1], block_c, start=True, stop=True)
                        nc.tensor.matmul(score[1][:, 0, 0:P], bv_w[:, n, :], wo[:, n, :], start=(n == 0), stop=False)
                    nc.tensor.matmul(score[1][:, 0, 0:P], c.ones_row[0:1, :], rows[0:1, 1, :],
                                     start=False, stop=True).then_inc(w_cols, 1)
                    pe.wait_ge(b_ready, 11)
                    for n in range(2):
                        ins = nc.tensor.matmul(score[1][:, 1, n:n + 1], rows_p[0:1, n, :], c.ones_row[0:1, 0:1],
                                               start=True, stop=True)
                    ins.then_inc(w_cols, 1)

        block = ctx.enter_context(nc.Block())

        @block.sync
        def _(sp):
            def load(i, u):
                sp.dma_start(x_sb[:, u, :, :], tiles_of(x_in, 2 * i + u)).then_inc(x_loaded[u], DMA)

            def place(n, i, u, stack, lo_ok, placed):
                sp.wait_ge(lo_ok, 2 * n + 2)
                sp.sem_inc(passed, 1)
                if positive(n - 1):
                    sp.wait_ge(s_done, T * (n - 1))
                    sp.sem_inc(passed, 1)
                if stack is k_st:
                    for part, src in enumerate(PARTS[1]):
                        sp.dma_start(k_st[32 * part:32 * part + 32, u, :, :], src[:, :]).then_inc(placed[u], DMA)
                else:
                    for h4 in range(4):
                        for part, src in enumerate(PARTS[0]):
                            r = 32 * part + 8 * h4
                            sp.dma_start(q_st[r:r + 8, u, :, h4, :], src[32 * h4:32 * h4 + 32, :]).then_inc(placed[u], DMA)

            def load_residual(n, i, u):
                if positive(n - 1):
                    sp.wait_ge(res_done, T * (n - 1))
                    sp.sem_inc(passed, 1)
                sp.dma_start(x_res[:, u, :, :], tiles_of(x_in, n)).then_inc(res_loaded[u], DMA)

            def store(n, u):
                sp.wait_ge(ln_done, T * n + T)
                sp.sem_inc(passed, 1)
                sp.dma_start(tiles_of(x_out, n), y[:, u, :, :]).then_inc(stored[u], DMA)

            def group(i, u):
                n = 2 * i + u
                ni, nu = next_group(i, u)
                if not (isinstance(n, int) and n >= GROUPS - 2):
                    sp.wait_ge(xT_ps, 2 * n + 4)
                    sp.sem_inc(passed, 1)
                    load(i + 1, u)
                if not is_last(n):
                    place(n + 1, ni, nu, q_st, q_lo_ok, q_placed)
                    load_residual(n + 1, ni, nu)
                    place(n + 1, ni, nu, k_st, k_lo_ok, k_placed)
                if positive(n):
                    store(n - 1, 1 - u)

            load(0, 1)
            load_residual(0, 0, 0)
            place(0, 0, 0, q_st, q_lo_ok, q_placed)
            place(0, 0, 0, k_st, k_lo_ok, k_placed)
            run_groups(sp, group)
            store(GROUPS - 1, 1)
            for u in range(2):
                sp.wait_ge(stored[u], DMA * GROUPS // 2)

        @block.gpsimd
        def _(pool):
            def low_prob(t, t2):
                pool.wait_ge(p_hi_ok, 2 * t + 2)
                nc.gpsimd.tensor_tensor(p_lo[64:128, t2, :, 1, :], prob[64:128, t2, :, :], p_hi[64:128, t2, :, 1, :],
                                        ALU.subtract).then_inc(p_lo1_ok, 1)

            def bias_residual(n, i, u, half):
                if half == 0:
                    pool.wait_ge(res_loaded[u], DMA * (i + 1))
                part = x_res[:, u, HALF * half:HALF * half + HALF, :]
                nc.gpsimd.tensor_tensor(part, part, bo_all[:, :].unsqueeze(1).to_broadcast([P, HALF, P]), ALU.add)\
                  .then_inc(res_biased, 1)

            def deviations(n, u):
                pool.wait_ge(mv_done, T * n + T)
                pool.sem_inc(passed, 1)
                nc.gpsimd.tensor_scalar(var_eps[:, :], mv[:, u, :, 1], LN_EPS, None, ALU.add).then_inc(eps_done, 1)
                pool.wait_ge(eps_done, n + 1)
                nc.gpsimd.tensor_tensor(rstd[:, :], var_eps[:, :], neg_half[:, :], ALU.pow).then_inc(rstd_done, 1)

            def layernorm(n, u, tiles):
                pool.wait_ge(rstd_done, n + 1)
                pool.sem_inc(passed, 1)
                for t in tiles:
                    nc.gpsimd.tensor_scalar(y[:, u, t, :], y[:, u, t, :], mv[:, u, t, 0:1], rstd[:, t:t + 1],
                                            ALU.subtract, ALU.mult).then_inc(ln_done, 1)

            def group(i, u):
                n = 2 * i + u
                for r in range(T):
                    low_prob(T * n + r, r % 2)
                    if r < 2 or positive(n):
                        if r != 2:
                            pool.wait_ge(p_lo1_ok, T * n + r + 1)
                            pool.sem_inc(passed, 1)
                        if r < 2:
                            bias_residual(n, i, u, r)
                            pool.wait_ge(res_biased, 2 * n + r + 1)
                        elif r == 3:
                            deviations(n - 1, 1 - u)
                            pool.wait_ge(rstd_done, n)
                        elif r > 3:
                            layernorm(n - 1, 1 - u, range(2 * r - 8, 2 * r - 6))
                            pool.wait_ge(ln_done, T * (n - 1) + 2 * r - 6)

            run_groups(pool, group)
            pool.wait_ge(p_lo1_ok, TILES)
            deviations(GROUPS - 1, 1)

        @block.scalar
        def _(act):
            def item(n, i, u, which, h):
                cols = slice(512 * h, 512 * h + 512)
                if which == 0:
                    act.wait_ge(xT_ps, 2 * n + h + 1)
                    nc.scalar.activation(xT[:, u, cols], bank[h][:, :], ACT.Copy).then_inc(xT_sb, 1)
                elif which == 1:
                    act.wait_ge(q_ps, 2 * n + h + 1)
                    if h == 0 and positive(n):
                        pi, pu = prev_group(i, u)
                        act.wait_ge(q_placed[pu], DMA * QPLACE * (pi + 1))
                    nc.scalar.activation(q_hi[:, cols], bank[h][:, :], ACT.Identity, bias=bcol[:, 0:1]).then_inc(q_hi_ok, 1)
                else:
                    act.wait_ge(k_ps, 2 * n + h + 1)
                    if h == 0 and positive(n):
                        pi, pu = prev_group(i, u)
                        act.wait_ge(k_placed[pu], DMA * KPLACE * (pi + 1))
                    nc.scalar.activation(k_hi[:, cols], bank[h][:, :], ACT.Identity, bias=bcol[:, 1:2]).then_inc(k_hi_ok, 1)

            def high_v(t, slot, k):
                act.wait_ge(v_ps, 2 * t + k + 1)
                if positive(t - 3):
                    act.wait_ge(av_done, 3 * (t - 3))
                nc.scalar.activation(v_hi[:, slot, 8 * k:8 * k + 8, 0:LATENT],
                                     bank[k][:, :].rearrange("p (h d) -> p h d", d=LATENT), ACT.Copy).then_inc(v_hi_ok, 1)

            def copy_oT(t, k):
                act.wait_ge(ot_ps, 2 * t + k + 1)
                if k == 0 and positive(t):
                    act.wait_ge(y_done, t)
                nc.scalar.activation(oT[:, 4 * k:4 * k + 4, :].rearrange("p c q -> p (c q)"), o_turned[:, :], ACT.Copy)\
                  .then_inc(ot_sb, 1)

            def exp(t, t2, slot, more_v):
                act.wait_ge(low_done, t + 1)
                if positive(t - 1):
                    act.wait_ge(p_lo0_ok, t - 1)
                    act.wait_ge(p_lo1_ok, t - 1)
                s = score[t2][:, :, :].rearrange("p a (h q) -> p (a h) q", q=S)
                nc.scalar.activation(prob[:, t2, :, :], s, ACT.Exp).then_inc(prob_ok, 1)
                if positive(t - 1):
                    copy_oT(t - 2, 1)
                if more_v:
                    high_v(t + 1, slot, 1)
                if positive(t - 1):
                    act.wait_ge(av_done, 3 * (t - 1))
                for b in range(2):
                    own = slice(64 * b, 64 * b + 64)
                    nc.scalar.activation(p_hi[own, t2, :, b, :], s[own], ACT.Exp).then_inc(p_hi_ok, 1)

            def group(i, u):
                n = 2 * i + u
                ni, nu = next_group(i, u)
                for r in range(T):
                    t = T * n + r
                    after = not (is_last(n) and r == T - 1)
                    items = r < 6 and not is_last(n)
                    if items and r % 2:
                        item(n + 1, ni, nu, r // 2, 1)
                    if positive(t - 1):
                        copy_oT(t - 2, 0)
                    if after:
                        high_v(t + 1, (r + 1) % 4, 0)
                    exp(t, r % 2, (r + 1) % 4, after)
                    if items and r % 2 == 0:
                        item(n + 1, ni, nu, r // 2, 0)

            for which in range(3):
                for h in range(2):
                    item(0, 0, 0, which, h)
            for k in range(2):
                high_v(0, 0, k)
            run_groups(act, group)
            for t in (TILES - 2, TILES - 1):
                for k in range(2):
                    copy_oT(t, k)

        @block.vector
        def _(dve):
            def item(n, which, h):
                cols = slice(512 * h, 512 * h + 512)
                if which == 1:
                    dve.wait_ge(q_hi_ok, 2 * n + h + 1)
                    nc.vector.scalar_tensor_tensor(out=q_lo[:, cols], in0=bank[h][:, :], scalar=bcol[:, 0:1], in1=q_hi[:, cols],
                                                   op0=ALU.add, op1=ALU.subtract).then_inc(q_lo_ok, 1)
                elif which == 2:
                    dve.wait_ge(k_hi_ok, 2 * n + h + 1)
                    nc.vector.scalar_tensor_tensor(out=k_lo[:, cols], in0=bank[h][:, :], scalar=bcol[:, 1:2], in1=k_hi[:, cols],
                                                   op0=ALU.add, op1=ALU.subtract).then_inc(k_lo_ok, 1)

            def low_v(t, slot, k):
                dve.wait_ge(v_hi_ok, 2 * t + k + 1)
                nc.vector.tensor_tensor(v_lo[:, slot, 8 * k:8 * k + 8, 0:LATENT],
                                        bank[k][:, :].rearrange("p (h d) -> p h d", d=LATENT),
                                        v_hi[:, slot, 8 * k:8 * k + 8, 0:LATENT], ALU.subtract).then_inc(v_lo_ok, 1)

            def row_max(t, t2):
                dve.wait_ge(s_done, t + 1)
                nc.vector.tensor_reduce(mt[:, :],
                                        score[t2][:, :, :].rearrange("p a (c q) -> p (a c) q", q=32),
                                        AX.X, ALU.max, apply_transpose=True).then_inc(max_done, 1)

            def spread_max(t, t2):
                dve.wait_ge(mt_done, t + 1)
                if positive(t):
                    dve.wait_ge(lower_done, t)
                nc.vector.tensor_reduce(mc[:, :], mt_ps.rearrange("p (k q) -> p q k", k=2), AX.X, ALU.max)\
                  .then_inc(mc_done, 1)
                dve.wait_ge(mc_done, t + 1)
                nc.vector.tensor_tensor(lower[0:64, t2, :, :], mc[:, :].unsqueeze(1).to_broadcast([64, 32, 32]),
                                        c.neg_own[0:64, :, :], ALU.mult).then_inc(lower_done, 1)

            def low_prob(t, t2):
                dve.wait_ge(p_hi_ok, 2 * t + 2)
                nc.vector.tensor_tensor(p_lo[0:64, t2, :, 0, :], prob[0:64, t2, :, :], p_hi[0:64, t2, :, 0, :],
                                        ALU.subtract).then_inc(p_lo0_ok, 1)

            def scale(t, t2):
                dve.wait_ge(av_done, 3 * t + 3)
                if positive(t):
                    dve.wait_ge(scaled, 3 * t)
                if positive(t - 1):
                    dve.wait_ge(ot_ps, 2 * t - 2)
                for g in (2, 0, 1):
                    nc.vector.reciprocal(recip[:, HEADS_OF[g].start:HEADS_OF[g].stop],
                                         values_of(t2, g)[:, :, LATENT]).then_inc(recip_done, 1)
                dve.wait_ge(recip_done, 3 * t + 3)
                for g in (2, 0, 1):
                    a, b = HEADS_OF[g].start, HEADS_OF[g].stop
                    nc.vector.tensor_tensor(o_sb[:, t2, a:b, :], values_of(t2, g)[:, :, 0:LATENT],
                                            recip[:, a:b].unsqueeze(2).to_broadcast([P, b - a, LATENT]), ALU.mult)\
                      .then_inc(scaled, 1)

            def residual(t, r, n, i, u):
                dve.wait_ge(y_done, t + 1)
                if r == 0:
                    dve.wait_ge(res_biased, 2 * n + 2)
                    if positive(n - 1):
                        dve.wait_ge(stored[u], DMA * i)
                nc.vector.tensor_tensor(y[:, u, r, :], y_ps, x_res[:, u, r, :], ALU.add).then_inc(res_done, 1)

            def tile_stats(t, r, u):
                dve.wait_ge(res_done, t + 1)
                nc.vector.bn_stats(stats[:, r, :], y[:, u, r, :]).then_inc(stat_done, 1)

            def tile_moments(t, r, n, u):
                if r == 0 and positive(n - 1):
                    dve.wait_ge(ln_done, T * (n - 1))
                    dve.sem_inc(passed, 1)
                dve.wait_ge(stat_done, t + 1)
                dve.sem_inc(passed, 1)
                nc.vector.bn_aggr(mv[:, u, r, :], stats[:, r, :]).then_inc(mv_done, 1)

            def group(i, u):
                n = 2 * i + u
                pi, pu = prev_group(i, u)
                for r in range(T):
                    t = T * n + r
                    after = not (is_last(n) and r == T - 1)
                    odd_items = r in (1, 3, 5) and not is_last(n)
                    row_max(t, r % 2)
                    if odd_items:
                        item(n + 1, r // 2, 0)
                    if positive(t):
                        low_prob(t - 1, (r + 1) % 2)
                    if r >= 3:
                        residual(t - 3, r - 3, n, i, u)
                    elif positive(n):
                        residual(t - 3, T + r - 3, n - 1, pi, pu)
                    if odd_items:
                        item(n + 1, r // 2, 1)
                    spread_max(t, r % 2)
                    if after:
                        low_v(t + 1, (r + 1) % 4, 0)
                    if positive(t):
                        scale(t - 1, (r + 1) % 2)
                    if r >= 4:
                        stats_of = (t - 4, r - 4, n, u)
                    else:
                        stats_of = (t - 4, T + r - 4, n - 1, pu)
                    if positive(t - 3):
                        tile_stats(stats_of[0], stats_of[1], stats_of[3])
                    if after:
                        low_v(t + 1, (r + 1) % 4, 1)
                    if positive(t - 3):
                        tile_moments(*stats_of)

            for which in range(3):
                for h in range(2):
                    item(0, which, h)
            for k in range(2):
                low_v(0, 0, k)
            run_groups(dve, group)
            low_prob(TILES - 1, 1)
            for t in (TILES - 3, TILES - 2, TILES - 1):
                if t == TILES - 2:
                    scale(TILES - 1, 1)
                residual(t, t % T, GROUPS - 1, GROUPS // 2 - 1, 1)
            for t in range(TILES - 4, TILES):
                tile_stats(t, t % T, 1)
            for t in range(TILES - 4, TILES):
                tile_moments(t, t % T, GROUPS - 1, 1)
            dve.wait_ge(rstd_done, GROUPS)
            for t in range(T):
                nc.vector.tensor_scalar(y[:, 1, t, :], y[:, 1, t, :], mv[:, 1, t, 0:1], rstd[:, t:t + 1],
                                        ALU.subtract, ALU.mult).then_inc(ln_done, 1)

        @block.tensor
        def _(pe):
            def item(n, i, u, which, h):
                out = bank[h]
                if which == 0:
                    pe.wait_ge(x_loaded[u], DMA * (i + 1))
                    for t in range(HALF):
                        ins = nc.tensor.transpose(out[:, P * t:P * t + P], x_sb[:, u, HALF * h + t, :], c.ident[:, :])
                    ins.then_inc(xT_ps, 1)
                else:
                    pe.wait_ge(xT_sb, 2 * n + h + 1)
                    nc.tensor.matmul(out[:, :], (wq_p, wk_p)[which - 1][:, :], xT[:, u, 512 * h:512 * h + 512],
                                     start=True, stop=True).then_inc((q_ps, k_ps)[which - 1], 1)

            ITEM_OUT = (xT_sb, q_lo_ok, k_lo_ok)

            def project_v(t, r, n, u, k):
                pe.wait_ge(xT_sb, 2 * n + r // HALF + 1)
                nc.tensor.matmul(bank[k][:, :], xT[:, u, P * r:P * r + P], wv[:, 512 * k:512 * k + 512],
                                 start=True, stop=True).then_inc(v_ps, 1)

            def scores(t, r, n, i, u):
                if r == 0:
                    pe.wait_ge(q_placed[u], DMA * QPLACE * (i + 1))
                    pe.wait_ge(k_placed[u], DMA * KPLACE * (i + 1))
                if positive(t - 1):
                    pe.wait_ge(scaled, 3 * (t - 1))
                s = score[r % 2]
                for half in range(2):
                    nc.tensor.matmul(s[:, half, :], c.ident_b[:, :], c.causal[:, :, :].rearrange("p h q -> p (h q)"),
                                     start=True, stop=False, skip_group_check=True)
                for f in range(4):
                    for b in range(2):
                        tok = slice(P * r + S * b, P * r + S * b + S)
                        ins = nc.tensor.matmul(s[64 * b:64 * b + 64, f // 2, 256 * (f % 2):256 * (f % 2) + 256],
                                               k_st[:, u, f, tok], q_st[:, u, f, :, tok],
                                               start=False, stop=False, skip_group_check=True)
                ins.then_inc(s_done, 1)

            def transpose_max(t):
                pe.wait_ge(max_done, t + 1)
                if positive(t - 2):
                    pe.wait_ge(res_done, t - 2)
                for b in range(2):
                    ins = nc.tensor.matmul(mt_ps[32 * b:32 * b + 32, :], mt[:, :], c.ident[:, 64 * b:64 * b + 64],
                                           start=True, stop=True)
                ins.then_inc(mt_done, 1)

            def lower_scores(t, t2):
                pe.wait_ge(lower_done, t + 1)
                for half in range(2):
                    ins = nc.tensor.matmul(score[t2][:, half, :], c.of_own[:, :],
                                           lower[:, t2, 16 * half:16 * half + 16, :].rearrange("p a q -> p (a q)"),
                                           start=False, stop=True, skip_group_check=True)
                ins.then_inc(low_done, 1)

            def values(t, t2, slot, maxima):
                pe.wait_ge(p_lo0_ok, t + 1)
                pe.wait_ge(p_lo1_ok, t + 1)
                pe.wait_ge(v_lo_ok, 2 * t + 2)
                for g, heads in enumerate(HEADS_OF):
                    if g == 2:
                        pe.wait_ge(mc_done, maxima)
                    out = values_of(t2, g)
                    for j, h in enumerate(heads):
                        hi = p_hi[:, t2, h, :, :].rearrange("p b q -> p (b q)")
                        lo = p_lo[:, t2, h, :, :].rearrange("p b q -> p (b q)")
                        nc.tensor.matmul(out[:, j, :], hi, v_hi[:, slot, h, :], start=True, stop=False)
                        nc.tensor.matmul(out[:, j, :], hi, v_lo[:, slot, h, :], start=False, stop=False)
                        ins = nc.tensor.matmul(out[:, j, :], lo, v_hi[:, slot, h, :], start=False, stop=True)
                    ins.then_inc(av_done, 1)

            def transpose_o(t, t2, k):
                pe.wait_ge(scaled, 3 * t + 3)
                if positive(2 * t + k):
                    pe.wait_ge(ot_sb, 2 * t + k)
                for m in range(HALF):
                    h = 2 * (HALF * k + m)
                    ins = nc.tensor.transpose(o_turned[:, P * m:P * m + P],
                                              o_sb[:, t2, h:h + 2, :].rearrange("p h d -> p (h d)"), c.ident[:, :])
                ins.then_inc(ot_ps, 1)

            def outputs(t, last=False):
                pe.wait_ge(ot_sb, 2 * t + 2)
                if not last:
                    pe.wait_ge(scaled, 3 * t + 4)
                else:
                    pe.wait_ge(res_done, t)
                for m in range(WO_CHUNKS):
                    ins = nc.tensor.matmul(y_ps, oT[:, m, :], wo[:, m, :], start=(m == 0), stop=(m == WO_CHUNKS - 1))
                ins.then_inc(y_done, 1)

            def group(i, u):
                n = 2 * i + u
                ni, nu = next_group(i, u)
                for r in range(T):
                    t, t2 = T * n + r, r % 2
                    after = not (is_last(n) and r == T - 1)
                    nr, v_n, v_u = (r + 1, n, u) if r < T - 1 else (0, n + 1, nu)
                    items = r < 6 and not is_last(n)
                    scores(t, r, n, i, u)
                    if items and t2:
                        pe.wait_ge(v_lo_ok, 2 * t + 2)
                        item(n + 1, ni, nu, r // 2, 1)
                    if positive(t - 2):
                        outputs(t - 3)
                    if positive(t - 1):
                        transpose_o(t - 2, t2, 0)
                    if after:
                        pe.wait_ge(v_lo_ok, 2 * t + 1)
                        if r in (1, 3, 5) and not is_last(n):
                            pe.wait_ge(ITEM_OUT[r // 2], 2 * (n + 1) + 1)
                        project_v(t + 1, nr, v_n, v_u, 0)
                    transpose_max(t)
                    if positive(t):
                        values(t - 1, 1 - t2, (r + 3) % 4, t + 1)
                    lower_scores(t, t2)
                    if positive(t - 1):
                        transpose_o(t - 2, t2, 1)
                    if after:
                        pe.wait_ge(v_lo_ok, 2 * t + 2)
                        if items and t2:
                            pe.wait_ge(ITEM_OUT[r // 2], 2 * (n + 1) + 2)
                        project_v(t + 1, nr, v_n, v_u, 1)
                    if items and t2 == 0:
                        pe.wait_ge(v_lo_ok, 2 * t + 3)
                        item(n + 1, ni, nu, r // 2, 0)

            for which in range(3):
                for h in range(2):
                    if which > 0:
                        pe.wait_ge(ITEM_OUT[which - 1], h + 1)
                    item(0, 0, 0, which, h)
            for k in range(2):
                pe.wait_ge(k_lo_ok, k + 1)
                project_v(0, 0, 0, 0, k)
            run_groups(pe, group)
            outputs(TILES - 3)
            transpose_o(TILES - 2, 0, 0)
            pe.wait_ge(res_done, TILES - 2)
            values(TILES - 1, 1, 3, TILES)
            transpose_o(TILES - 2, 0, 1)
            outputs(TILES - 2)
            for k in range(2):
                transpose_o(TILES - 1, 1, k)
            outputs(TILES - 1, last=True)


E_HID = 32
ROWS = 2
PER_ROW = P // E_HID


def top1_experts(nc, c, tag, x_in, x_out, w):
    STEPS = TILES // HALF
    with ExitStack() as ctx:
        def sb(name, shape, dt=F32):
            return ctx.enter_context(nc.sbuf_tensor(f"{tag}_{name}", shape, dt))

        def ps(name, shape):
            return ctx.enter_context(nc.psum_tensor(f"{tag}_{name}", shape, F32))

        sem = ctx.enter_context(Semaphores(nc, tag))

        def sem2(name):
            return [sem(f"{name}{u}") for u in range(2)]

        gate_rows = sb("gate_rows", [32, P])
        gate_cols = sb("gate_cols", [P, 32])
        w1 = sb("w1", [P, EXPERTS, E_HID])
        w1_s = sb("w1_s", [P, EXPERTS * E_HID])
        b1_row = sb("b1_row", [1, EXPERTS * E_HID])
        b1_part = sb("b1_part", [P, ROWS])
        b1_col = sb("b1_col", [P, ROWS])
        w2 = sb("w2", [P, ROWS, P])
        b2 = sb("b2", [32, P])
        spread = sb("spread", [32, ROWS, PER_ROW, E_HID], BF16)
        rank = sb("rank", [P, EXPERTS])
        neg_half = sb("neg_half", [P, HALF])

        x_sb = sb("x", [P, 2, HALF, P])
        x_hat = sb("x_hat", [P, 2, HALF, P])
        xT, xhT = sb("xT", [P, 2, HALF * P]), sb("xhT", [P, 2, HALF * P])
        top, best = sb("top", [P, HALF]), sb("best", [P, HALF])
        is_top = sb("is_top", [P, HALF, EXPERTS])
        one_hot = sb("one_hot", [P, HALF, 32], BF16)
        hot = sb("hot", [32, 2, HALF * P])
        hot_b = sb("hot_b", [32, HALF * P], BF16)
        hid = sb("hid", [P, ROWS, HALF * P])
        own = sb("own", [P, 2, ROWS, HALF * P])
        x_res = sb("x_res", [P, 2, HALF, P])
        y = sb("y", [P, 2, HALF, P])
        stats_in, stats = sb("stats_in", [P, HALF, 6]), sb("stats", [P, HALF, 6])
        mv_in, mv = sb("mv_in", [P, HALF, 2]), sb("mv", [P, 2, HALF, 2])
        var_eps, rstd = sb("var_eps", [P, HALF]), sb("rstd", [P, HALF])
        in_var, in_scale = sb("in_var", [P, HALF]), sb("in_scale", [P, HALF])

        turned = ps("turned", [P, 512])
        l_ps = ps("l_ps", [P, 512])
        hot_ps = ps("hot_ps", [P, 512])
        h_ps = [ps(f"h_ps{k}", [P, 512]) for k in range(ROWS)]
        m_ps = [ps(f"m_ps{k}", [P, 512]) for k in range(ROWS)]
        y_ps = ps("y_ps", [P, 512])

        w_loaded, filled, picked, cols, biased = map(sem, ("w_loaded", "filled", "picked", "cols", "biased"))
        x_loaded, res_loaded, stored = map(sem2, ("x_loaded", "res_loaded", "stored"))
        x_ps, xh_ps, l_done, hot_done, h_done, m_done, y_done = map(
            sem, ("x_ps", "xh_ps", "l_done", "hot_done", "h_done", "m_done", "y_done"))
        xT_sb, xhT_sb, hot_sb, gelu_done = map(sem, ("xT_sb", "xhT_sb", "hot_sb", "gelu_done"))
        in_stats, in_mv, routed, hot_b_sb, own_done = map(sem, ("in_stats", "in_mv", "routed", "hot_b_sb", "own_done"))
        res_done, stat_done, mv_done = map(sem, ("res_done", "stat_done", "mv_done"))
        in_eps, in_rstd, x_hat_done, eps_done, rstd_done, ln_done = map(
            sem, ("in_eps", "in_rstd", "x_hat_done", "eps_done", "rstd_done", "ln_done"))
        passed = sem("passed")

        with nc.Block() as block:
            @block.sync
            def _(sp):
                sp.dma_start(w1[:, :, :], w["W1"].rearrange("e d f -> d e f")).then_inc(w_loaded, DMA)
                sp.dma_start(b1_row[:, :], w["b1"].rearrange("(a e) f -> a (e f)", a=1)).then_inc(w_loaded, DMA)
                sp.dma_start(w2[:, :, :], w["W2"].rearrange("(c e) f d -> (e f) c d", c=ROWS)).then_inc(w_loaded, DMA)
                sp.wait_ge(filled, 2)
                for n, name in enumerate(("ln_scale", "ln_bias", "Wg")):
                    sp.dma_start(gate_rows[EXPERTS * n:EXPERTS * n + EXPERTS, :], w[name]).then_inc(w_loaded, DMA)
                sp.dma_start(b2[0:EXPERTS, :], w["b2"]).then_inc(w_loaded, DMA)
                for m in range(2):
                    sp.dma_start(x_sb[:, m, :, :], quarter_tiles(x_in, m)).then_inc(x_loaded[m], DMA)
                sp.wait_ge(w_loaded, 7 * DMA)

            @block.gpsimd
            def _(pool):
                pool.wait_ge(filled, 3)
                nc.gpsimd.affine_select(out=spread[:, :, :, :], in_=spread[:, :, :, :], compare_op=ALU.not_equal,
                                        fill=1.0, base=0, pattern=[[-PER_ROW, ROWS], [-1, PER_ROW], [0, E_HID]],
                                        channel_multiplier=1).then_inc(picked, 1)
                pool.wait_ge(picked, 1)

            @block.vector
            def _(dve):
                nc.vector.memset(gate_rows[:, :], 0.0).then_inc(filled, 1)
                nc.vector.memset(b2[:, :], 0.0).then_inc(filled, 1)
                nc.vector.memset(spread[:, :, :, :], 0.0).then_inc(filled, 1)
                nc.vector.memset(one_hot[:, :, :], 0.0).then_inc(filled, 1)
                nc.vector.memset(neg_half[:, :], -0.5).then_inc(filled, 1)
                for e in range(EXPERTS):
                    nc.vector.memset(rank[:, e:e + 1], float(EXPERTS - e)).then_inc(filled, 1)
                dve.wait_ge(cols, 1)
                nc.vector.tensor_copy(gate_cols[:, :], l_ps[:, 0:32]).then_inc(biased, 1)
                nc.vector.tensor_copy(b1_part[:, :], y_ps[:, 0:ROWS]).then_inc(biased, 1)
                dve.wait_ge(biased, 2)
                nc.vector.tensor_tensor(w1_s[:, :].rearrange("p (e f) -> p e f", f=E_HID), w1[:, :, :],
                                        gate_cols[:, 0:EXPERTS].unsqueeze(2).to_broadcast([P, EXPERTS, E_HID]),
                                        ALU.mult).then_inc(biased, 1)
                dve.wait_ge(cols, 2)
                nc.vector.tensor_tensor(b1_col[:, :], m_ps[0][:, 0:ROWS], b1_part[:, :], ALU.add).then_inc(biased, 1)

            @block.tensor
            def _(pe):
                pe.wait_ge(w_loaded, 7 * DMA)
                nc.tensor.transpose(l_ps[:, 0:32], gate_rows[:, :], c.ident[0:32, 0:32])
                for k in range(ROWS):
                    ins = nc.tensor.matmul(y_ps[:, k:k + 1], b1_row[0:1, P * k:P * k + P], c.ones_row[0:1, 0:1],
                                           start=True, stop=True)
                ins.then_inc(cols, 1)
                pe.wait_ge(biased, 2)
                for e in range(EXPERTS):
                    r, k = E_HID * (e % PER_ROW), e // PER_ROW
                    ins = nc.tensor.matmul(m_ps[0][r:r + E_HID, k:k + 1], w1[:, e, :],
                                           gate_cols[:, EXPERTS + e:EXPERTS + e + 1], start=True, stop=True)
                ins.then_inc(cols, 1)

        block = ctx.enter_context(nc.Block())

        def run(eng, step, ahead=3):
            rounds = (STEPS - ahead) // 2
            for k in range(-3, 2):
                step(Turn(0, k))
            with eng.Fori(1, rounds) as i:
                for u in range(2):
                    step(Turn(i, u))
            for k in range(2 * rounds, STEPS + 1):
                step(Turn(0, k))

        @block.sync
        def _(sp):
            def load_x(m):
                if m.from_(2):
                    sp.wait_ge(xh_ps, m.n - 1)
                    sp.sem_inc(passed, 1)
                    sp.dma_start(x_sb[:, m.u, :, :], quarter_tiles(x_in, m.n)).then_inc(x_loaded[m.u], DMA)

            def load_res(m):
                if m.from_(2):
                    sp.wait_ge(res_done, m.n - 1)
                    sp.sem_inc(passed, 1)
                sp.dma_start(x_res[:, m.u, :, :], quarter_tiles(x_in, m.n)).then_inc(res_loaded[m.u], DMA)

            def store(m):
                sp.wait_ge(ln_done, HALF * (m.n + 1))
                sp.sem_inc(passed, 1)
                sp.dma_start(quarter_tiles(x_out, m.n), y[:, m.u, :, :]).then_inc(stored[m.u], DMA)

            def step(s):
                if s.after(3).live(STEPS):
                    load_x(s.after(3))
                if s.after(1).live(STEPS):
                    load_res(s.after(1))
                if s.after(-2).live(STEPS):
                    store(s.after(-2))

            run(sp, step)
            store(Turn(0, STEPS - 1))
            for u in range(2):
                sp.wait_ge(stored[u], DMA * STEPS // 2)

        @block.gpsimd
        def _(pool):
            def inner_rstd(m):
                pool.wait_ge(in_mv, m.n + 1)
                pool.sem_inc(passed, 1)
                nc.gpsimd.tensor_scalar(in_var[:, :], mv_in[:, :, 1], LN_EPS, None, ALU.add).then_inc(in_eps, 1)
                pool.wait_ge(in_eps, m.n + 1)
                nc.gpsimd.tensor_tensor(in_scale[:, :], in_var[:, :], neg_half[:, :], ALU.pow).then_inc(in_rstd, 1)

            def layernorm(m):
                pool.wait_ge(mv_done, m.n + 1)
                pool.sem_inc(passed, 1)
                nc.gpsimd.tensor_scalar(var_eps[:, :], mv[:, m.u, :, 1], LN_EPS, None, ALU.add).then_inc(eps_done, 1)
                pool.wait_ge(eps_done, m.n + 1)
                if m.from_(1):
                    pool.wait_ge(ln_done, HALF * m.n)
                nc.gpsimd.tensor_tensor(rstd[:, :], var_eps[:, :], neg_half[:, :], ALU.pow).then_inc(rstd_done, 1)
                if isinstance(m.n, int) and m.n == STEPS - 1:
                    return
                pool.wait_ge(rstd_done, m.n + 1)
                pool.sem_inc(passed, 1)
                for t in range(HALF):
                    nc.gpsimd.tensor_scalar(y[:, m.u, t, :], y[:, m.u, t, :], mv[:, m.u, t, 0:1], rstd[:, t:t + 1],
                                            ALU.subtract, ALU.mult).then_inc(ln_done, 1)

            def step(s):
                if s.after(2).live(STEPS):
                    inner_rstd(s.after(2))
                if s.after(-1).live(STEPS):
                    layernorm(s.after(-1))

            run(pool, step)

        @block.scalar
        def _(act):
            def copy_xT(m):
                act.wait_ge(x_ps, m.n + 1)
                if m.from_(2):
                    act.wait_ge(l_done, m.n - 1)
                nc.scalar.activation(xT[:, m.u, :], turned[:, :], ACT.Copy).then_inc(xT_sb, 1)

            def copy_xhT(m):
                act.wait_ge(xh_ps, m.n + 1)
                if m.from_(2):
                    act.wait_ge(h_done, ROWS * (m.n - 1))
                nc.scalar.activation(xhT[:, m.u, :], turned[:, :], ACT.Copy).then_inc(xhT_sb, 1)

            def copy_hot(m):
                act.wait_ge(hot_done, m.n + 1)
                if m.from_(2):
                    act.wait_ge(y_done, m.n - 1)
                    act.wait_ge(hot_b_sb, m.n - 1)
                nc.scalar.activation(hot[:, m.u, :], hot_ps[0:32, :], ACT.Copy).then_inc(hot_sb, 1)

            def gelu(m):
                if m.from_(1):
                    act.wait_ge(own_done, ROWS * m.n)
                for k in range(ROWS):
                    act.wait_ge(h_done, ROWS * m.n + k + 1)
                    nc.scalar.activation(hid[:, k, :], h_ps[k][:, :], ACT.Gelu, bias=b1_col[:, k:k + 1])\
                      .then_inc(gelu_done, 1)

            def step(s):
                if s.after(1).live(STEPS):
                    copy_xT(s.after(1))
                if s.live(STEPS):
                    copy_hot(s)
                    gelu(s)
                if s.after(1).live(STEPS):
                    copy_xhT(s.after(1))

            run(act, step)

        @block.vector
        def _(dve):
            def inner_moments(m):
                dve.wait_ge(x_loaded[m.u], DMA * (m.i + 1))
                if m.from_(1):
                    dve.wait_ge(in_mv, m.n)
                    dve.sem_inc(passed, 1)
                for t in range(HALF):
                    nc.vector.bn_stats(stats_in[:, t, :], x_sb[:, m.u, t, :]).then_inc(in_stats, 1)
                dve.wait_ge(in_stats, HALF * (m.n + 1))
                dve.sem_inc(passed, 1)
                if m.from_(1):
                    dve.wait_ge(x_hat_done, HALF * m.n)
                    dve.sem_inc(passed, 1)
                for t in range(HALF):
                    ins = nc.vector.bn_aggr(mv_in[:, t, :], stats_in[:, t, :])
                ins.then_inc(in_mv, 1)

            def normalise_inputs(m):
                dve.wait_ge(in_rstd, m.n + 1)
                dve.sem_inc(passed, 1)
                if m.from_(2):
                    dve.wait_ge(xh_ps, m.n - 1)
                    dve.sem_inc(passed, 1)
                for t in range(HALF):
                    nc.vector.tensor_scalar(x_hat[:, m.u, t, :], x_sb[:, m.u, t, :], mv_in[:, t, 0:1],
                                            in_scale[:, t:t + 1], ALU.subtract, ALU.mult).then_inc(x_hat_done, 1)

            def route(m):
                lg = l_ps[:, 0:HALF * EXPERTS].rearrange("p (t e) -> p t e", e=EXPERTS)
                shape = [P, HALF, EXPERTS]
                dve.wait_ge(l_done, m.n + 1)
                nc.vector.tensor_reduce(top[:, :], lg, AX.X, ALU.max).then_inc(routed, 1)
                dve.wait_ge(routed, 5 * m.n + 1)
                nc.vector.tensor_tensor(is_top[:, :, :], lg, top[:, :].unsqueeze(2).to_broadcast(shape), ALU.is_ge)\
                  .then_inc(routed, 1)
                dve.wait_ge(routed, 5 * m.n + 2)
                nc.vector.tensor_tensor(is_top[:, :, :], is_top[:, :, :], rank[:, :].unsqueeze(1).to_broadcast(shape),
                                        ALU.mult).then_inc(routed, 1)
                dve.wait_ge(routed, 5 * m.n + 3)
                nc.vector.tensor_reduce(best[:, :], is_top[:, :, :], AX.X, ALU.max).then_inc(routed, 1)
                dve.wait_ge(routed, 5 * m.n + 4)
                if m.from_(1):
                    dve.wait_ge(hot_done, m.n)
                nc.vector.tensor_tensor(one_hot[:, :, 0:EXPERTS], rank[:, :].unsqueeze(1).to_broadcast(shape),
                                        best[:, :].unsqueeze(2).to_broadcast(shape), ALU.is_equal).then_inc(routed, 1)

            def copy_hot_b(m):
                dve.wait_ge(hot_sb, m.n + 1)
                if m.from_(1):
                    dve.wait_ge(m_done, m.n)
                nc.vector.tensor_copy(hot_b[:, :], hot[:, m.u, :]).then_inc(hot_b_sb, 1)

            def mask(m):
                dve.wait_ge(m_done, m.n + 1)
                dve.wait_ge(gelu_done, ROWS * (m.n + 1))
                if m.from_(2):
                    dve.wait_ge(y_done, m.n - 1)
                for k in range(ROWS):
                    nc.vector.tensor_tensor(own[:, m.u, k, :], hid[:, k, :], m_ps[k][:, :], ALU.mult).then_inc(own_done, 1)

            def residual(m):
                dve.wait_ge(y_done, m.n + 1)
                dve.wait_ge(res_loaded[m.u], DMA * (m.i + 1))
                if m.from_(2):
                    dve.wait_ge(stored[m.u], DMA * m.i)
                nc.vector.tensor_tensor(y[:, m.u, :, :], y_ps[:, :].rearrange("p (t d) -> p t d", d=P),
                                        x_res[:, m.u, :, :], ALU.add).then_inc(res_done, 1)

            def moments(m):
                dve.wait_ge(res_done, m.n + 1)
                if m.from_(1):
                    dve.wait_ge(mv_done, m.n)
                for t in range(HALF):
                    nc.vector.bn_stats(stats[:, t, :], y[:, m.u, t, :]).then_inc(stat_done, 1)
                dve.wait_ge(stat_done, HALF * (m.n + 1))
                dve.sem_inc(passed, 1)
                if m.from_(2):
                    dve.wait_ge(ln_done, HALF * (m.n - 1))
                    dve.sem_inc(passed, 1)
                for t in range(HALF):
                    ins = nc.vector.bn_aggr(mv[:, m.u, t, :], stats[:, t, :])
                ins.then_inc(mv_done, 1)

            def step(s):
                if s.live(STEPS):
                    copy_hot_b(s)
                if s.after(1).live(STEPS):
                    normalise_inputs(s.after(1))
                if s.after(-1).live(STEPS):
                    residual(s.after(-1))
                if s.live(STEPS):
                    mask(s)
                if s.after(1).live(STEPS):
                    route(s.after(1))
                if s.after(2).live(STEPS):
                    inner_moments(s.after(2))
                if s.after(-1).live(STEPS):
                    moments(s.after(-1))

            run(dve, step)

            m = Turn(0, STEPS - 1)
            dve.wait_ge(rstd_done, STEPS)
            for t in range(HALF):
                nc.vector.tensor_scalar(y[:, m.u, t, :], y[:, m.u, t, :], mv[:, m.u, t, 0:1], rstd[:, t:t + 1],
                                        ALU.subtract, ALU.mult).then_inc(ln_done, 1)

        @block.tensor
        def _(pe):
            def turn_x(m):
                pe.wait_ge(x_loaded[m.u], DMA * (m.i + 1))
                if m.from_(1):
                    pe.wait_ge(xhT_sb, m.n)
                for t in range(HALF):
                    ins = nc.tensor.transpose(turned[:, P * t:P * t + P], x_sb[:, m.u, t, :], c.ident[:, :])
                ins.then_inc(x_ps, 1)

            def turn_x_hat(m):
                pe.wait_ge(x_hat_done, HALF * (m.n + 1))
                pe.wait_ge(xT_sb, m.n + 1)
                for t in range(HALF):
                    ins = nc.tensor.transpose(turned[:, P * t:P * t + P], x_hat[:, m.u, t, :], c.ident[:, :])
                ins.then_inc(xh_ps, 1)

            def logits(m):
                pe.wait_ge(xT_sb, m.n + 1)
                if m.from_(1):
                    pe.wait_ge(routed, 5 * m.n)
                for t in range(HALF):
                    ins = nc.tensor.matmul(l_ps[:, EXPERTS * t:EXPERTS * t + EXPERTS], xT[:, m.u, P * t:P * t + P],
                                           gate_cols[:, 2 * EXPERTS:3 * EXPERTS], start=True, stop=True)
                ins.then_inc(l_done, 1)

            def turn_hot(m):
                pe.wait_ge(routed, 5 * m.n + 5)
                if m.from_(1):
                    pe.wait_ge(hot_sb, m.n)
                for t in range(HALF):
                    ins = nc.tensor.matmul(hot_ps[0:32, P * t:P * t + P], one_hot[:, t, :], c.ident_b[:, :],
                                           start=True, stop=True)
                ins.then_inc(hot_done, 1)

            def masks(m):
                pe.wait_ge(hot_b_sb, m.n + 1)
                if m.from_(1):
                    pe.wait_ge(own_done, ROWS * m.n)
                for k in range(ROWS):
                    ins = nc.tensor.matmul(m_ps[k][:, :], spread[:, k, :, :].rearrange("p e f -> p (e f)"), hot_b[:, :],
                                           start=True, stop=True)
                ins.then_inc(m_done, 1)

            def hidden(m):
                pe.wait_ge(xhT_sb, m.n + 1)
                if m.from_(1):
                    pe.wait_ge(gelu_done, ROWS * m.n)
                for k in range(ROWS):
                    nc.tensor.matmul(h_ps[k][:, :], w1_s[:, P * k:P * k + P], xhT[:, m.u, :],
                                     start=True, stop=True).then_inc(h_done, 1)

            def outputs(m):
                pe.wait_ge(own_done, ROWS * (m.n + 1))
                pe.wait_ge(hot_sb, m.n + 1)
                if m.from_(1):
                    pe.wait_ge(res_done, m.n)
                for t in range(HALF):
                    tok = slice(P * t, P * t + P)
                    for k in range(ROWS):
                        nc.tensor.matmul(y_ps[:, tok], own[:, m.u, k, tok], w2[:, k, :], start=(k == 0), stop=False)
                    ins = nc.tensor.matmul(y_ps[:, tok], hot[:, m.u, tok], b2[:, :], start=False, stop=True)
                ins.then_inc(y_done, 1)

            def step(s):
                if s.after(1).live(STEPS):
                    turn_x(s.after(1))
                if s.live(STEPS):
                    hidden(s)
                    turn_hot(s)
                if s.after(-1).live(STEPS):
                    outputs(s.after(-1))
                if s.live(STEPS):
                    masks(s)
                if s.after(1).live(STEPS):
                    turn_x_hat(s.after(1))
                    logits(s.after(1))

            run(pe, step)


_INS = ["x", "ctx_1024",
        "L0_attn_Wq", "L0_attn_bq", "L0_attn_Wk", "L0_attn_bk", "L0_attn_Wv", "L0_attn_bv", "L0_attn_Wo", "L0_attn_bo",
        "L0_attn_m",
        "L0_xattn_Wq", "L0_xattn_bq", "L0_xattn_Wk", "L0_xattn_bk", "L0_xattn_Wv", "L0_xattn_bv", "L0_xattn_Wo",
        "L0_xattn_bo",
        "L0_ffn_gate_w", "L0_ffn_gate_b", "L0_ffn_w1", "L0_ffn_b1", "L0_ffn_w2", "L0_ffn_b2",
        "L1_attn_Wq", "L1_attn_bq", "L1_attn_Wk", "L1_attn_bk", "L1_attn_Wv", "L1_attn_bv", "L1_attn_Wo", "L1_attn_bo",
        "L1_attn_Wc",
        "L1_xattn_Wq", "L1_xattn_bq", "L1_xattn_Wk", "L1_xattn_bk", "L1_xattn_Wv", "L1_xattn_bv", "L1_xattn_Wo",
        "L1_xattn_bo",
        "L1_ffn_Wg", "L1_ffn_ln_scale", "L1_ffn_ln_bias", "L1_ffn_W1", "L1_ffn_b1", "L1_ffn_W2", "L1_ffn_b2"]
_OUTS = [((B, S, D), "float32")]


def decoder_kernel(nc, a, out):
    def weights(prefix):
        return {name[len(prefix):]: ap for name, ap in a.items() if name.startswith(prefix)}

    def tokens(name):
        return nc.dram_tensor(name, [B * S, D], F32, kind="Internal").ap()

    x0, ctx_in = (a[n].rearrange("b s d -> (b s) d") for n in ("x", "ctx_1024"))
    x1, x2, x3, x4, x5 = (tokens(f"after_{n}") for n in ("l0_attn", "l0_xattn", "l0_ffn", "l1_attn", "l1_xattn"))
    with ExitStack() as ctx:
        c = Constants(nc, ctx)
        make_constants(nc, c)
        linear_attention(nc, c, "l0_attn", x0, x1, weights("L0_attn_"))
        cross_attention(nc, c, "l0_xattn", x1, ctx_in, x2, weights("L0_xattn_"), causal=True)
        moe_layer(nc, c, "l0_ffn", x2, x3, weights("L0_ffn_"))
        latent_attention(nc, c, "l1_attn", x3, x4, weights("L1_attn_"))
        cross_attention(nc, c, "l1_xattn", x4, ctx_in, x5, weights("L1_xattn_"), causal=False)
        top1_experts(nc, c, "l1_ffn", x5, out.rearrange("b s d -> (b s) d"), weights("L1_ffn_"))


def kernel(**inputs):
    import numpy as _np
    import concourse.bacc as _bacc
    from concourse import mybir as _mybir
    from concourse.bass_utils import run_bass_kernel_spmd as _run

    nc = _bacc.Bacc("TRN2", target_bir_lowering=False, num_devices=1)
    arrays, args = {}, {}
    for name in _INS:
        arr = _np.ascontiguousarray(inputs[name])
        arrays[f"in_{name}_dram"] = arr
        args[name] = nc.dram_tensor(f"in_{name}_dram", arr.shape, _mybir.dt.from_np(arr.dtype), kind="ExternalInput").ap()
    (shape, dtype), = _OUTS
    out = nc.dram_tensor("out_0_dram", shape, _mybir.dt.from_np(_np.dtype(dtype)), kind="ExternalOutput").ap()
    decoder_kernel(nc, args, out)
    r = _run(nc, [arrays], core_ids=[0])
    return r.results[0]["out_0_dram"]
```
